# Optimizing a Trainium2 kernel written in Bass

```python
import numpy as np
import jax
import jax.numpy as jnp

def _softmax(x, axis=-1):
    return jax.nn.softmax(x, axis=axis)

def _gelu(x):
    return jax.nn.gelu(x, approximate=True)

def _silu(x):
    return jax.nn.silu(x)

def _sigmoid(x):
    return jax.nn.sigmoid(x)

def _layernorm(x, axis=-1, eps=1e-05):
    m = jnp.mean(x, axis=axis, keepdims=True)
    v = jnp.var(x, axis=axis, keepdims=True)
    return (x - m) / jnp.sqrt(v + eps)

def _scatter_add(tgt, idx, src, axis=0):
    return tgt.at[idx].add(src)

def _segment_sum(src, seg, n):
    return jax.ops.segment_sum(src, seg, n)
kernel_name = 'mk_cond_resid_d2_seqx_r2_4dc504'

def setup_inputs(seed: int=0):
    np.random.seed(seed)
    _w = jnp.asarray

    def _rec_inputs():
        import jax
        import jax.numpy as jnp
        _rk = jax.random.key(seed)
        x = -7.109e-05 + 0.9999 * jax.random.normal(jax.random.fold_in(_rk, 1), (8, 1024, 512), jnp.float32)
        _lenS = 1024 - jax.random.randint(jax.random.fold_in(_rk, 7), (8,), 0, max(1, 1024 // 4) + 1, jnp.int32)
        _lenS2 = 1024 - jax.random.randint(jax.random.fold_in(_rk, 8), (8,), 0, max(1, 1024 // 4) + 1, jnp.int32)
        itok_B_0_8 = jax.random.randint(jax.random.fold_in(_rk, 11), (8,), 0, 9, jnp.int32)
        condB_tauraws = -5.74692 + 0.777674 * jax.random.normal(jax.random.fold_in(_rk, 12), (8,), jnp.float32)
        cond_256 = -0.000235209 + 0.019331 * jax.random.normal(jax.random.fold_in(_rk, 13), (8, 128), jnp.float32)
        condB_bn2 = jnp.zeros((8,), jnp.float32)
        cond_1024 = -4.10585e-05 + 0.0199478 * jax.random.normal(jax.random.fold_in(_rk, 15), (8, 512), jnp.float32)
        return (x, itok_B_0_8, condB_tauraws, cond_256, condB_bn2, cond_1024)
    x, itok_B_0_8, condB_tauraws, cond_256, condB_bn2, cond_1024 = _rec_inputs()

    def _L0_cond_setup():
        import jax, jax.numpy as jnp
        import numpy as np
        LN_EPS = 1e-05
        key = jax.random.key(seed)
        ks = jax.random.split(key, 8)
        B, S, H, A, L = (32, 1024, 512, 128, 10)
        return {'hidden_states': jax.random.normal(ks[0], (B, S, H), dtype=jnp.float32), 'language_ids': jax.random.randint(ks[1], (B,), 0, L, dtype=jnp.int64), 'W1': jax.random.normal(ks[2], (L, H, A), dtype=jnp.float32) * (1.0 / np.sqrt(H)), 'b1': jnp.zeros((L, A), dtype=jnp.float32), 'W2': jax.random.normal(ks[3], (L, A, H), dtype=jnp.float32) * (1.0 / np.sqrt(A)), 'b2': jnp.zeros((L, H), dtype=jnp.float32), 'gamma': jnp.ones((L, H), dtype=jnp.float32), 'beta': jnp.zeros((L, H), dtype=jnp.float32)}
    _L0_cond_all = _L0_cond_setup()
    _L0_cond_in = {k: v for k, v in _L0_cond_all.items() if k in ('W1', 'b1', 'W2', 'b2', 'gamma', 'beta')}
    del _L0_cond_all

    def _L1_cond_setup():
        import jax, jax.numpy as jnp
        import numpy as np
        import math
        B, T, E, D = (4, 1024, 512, 4)

        def _tau_init(t):
            a = 0.1 ** (1.0 / max(t - 1, 1))
            tt = -math.log(max(a, 1e-10))
            return math.log(math.exp(tt) - 1 + 1e-10)

        def causal_ema(b, tau_raw):
            alpha = jnp.exp(-jax.nn.softplus(tau_raw)).astype(b.dtype)

            def step(h, bt):
                h = alpha * h + bt
                return (h, h)
            h0 = jnp.zeros((b.shape[0], b.shape[2]), b.dtype)
            _, hs = jax.lax.scan(step, h0, jnp.swapaxes(b, 0, 1))
            return jnp.swapaxes(hs, 0, 1)
        key = jax.random.key(seed)
        ks = jax.random.split(key, 10)
        s = 0.02
        return {'x': jax.random.normal(ks[0], (B, T, E), jnp.float32), 'tau_ctx': jnp.float32(_tau_init(max(T // 2, 4))), 'tau_raws': jnp.array([_tau_init(max(T // 2 ** i, 2)) for i in range(D)], jnp.float32), 'Wg': jax.random.normal(ks[1], (E, 2 * E), jnp.float32) * s, 'bg': jnp.full((E,), -0.5, jnp.float32), 'Wn1': jax.random.normal(ks[2], (E // 4, E), jnp.float32) * s, 'bn1': jnp.zeros((E // 4,), jnp.float32), 'Wn2': jax.random.normal(ks[3], (D, E // 4), jnp.float32) * s, 'bn2': jnp.zeros((D,), jnp.float32), 'blend': jax.random.normal(ks[4], (D, E), jnp.float32) * s, 'Wsoma': jax.random.normal(ks[5], (E, E), jnp.float32) * s, 'bsoma': jnp.zeros((E,), jnp.float32), 'Wtemp': jax.random.normal(ks[6], (E, E), jnp.float32) * s, 'btemp': jnp.zeros((E,), jnp.float32), 'Wout': jax.random.normal(ks[7], (E, E), jnp.float32) * s, 'gamma': jnp.ones((E,), jnp.float32), 'beta': jnp.zeros((E,), jnp.float32)}
    _L1_cond_all = _L1_cond_setup()
    _L1_cond_in = {k: v for k, v in _L1_cond_all.items() if k in ('tau_ctx', 'Wg', 'bg', 'Wn1', 'bn1', 'Wsoma', 'bsoma', 'Wtemp', 'btemp', 'Wout', 'gamma', 'beta')}
    del _L1_cond_all
    return {'x': x, 'itok_B_0_8': itok_B_0_8, 'condB_tauraws': condB_tauraws, 'cond_256': cond_256, 'condB_bn2': condB_bn2, 'cond_1024': cond_1024, 'L0_cond_W1': _L0_cond_in['W1'], 'L0_cond_b1': _L0_cond_in['b1'], 'L0_cond_W2': _L0_cond_in['W2'], 'L0_cond_b2': _L0_cond_in['b2'], 'L0_cond_gamma': _L0_cond_in['gamma'], 'L0_cond_beta': _L0_cond_in['beta'], 'L1_cond_tau_ctx': _L1_cond_in['tau_ctx'], 'L1_cond_Wg': _L1_cond_in['Wg'], 'L1_cond_bg': _L1_cond_in['bg'], 'L1_cond_Wn1': _L1_cond_in['Wn1'], 'L1_cond_bn1': _L1_cond_in['bn1'], 'L1_cond_Wsoma': _L1_cond_in['Wsoma'], 'L1_cond_bsoma': _L1_cond_in['bsoma'], 'L1_cond_Wtemp': _L1_cond_in['Wtemp'], 'L1_cond_btemp': _L1_cond_in['btemp'], 'L1_cond_Wout': _L1_cond_in['Wout'], 'L1_cond_gamma': _L1_cond_in['gamma'], 'L1_cond_beta': _L1_cond_in['beta']}

def reference(x, itok_B_0_8, condB_tauraws, cond_256, condB_bn2, cond_1024, L0_cond_W1, L0_cond_b1, L0_cond_W2, L0_cond_b2, L0_cond_gamma, L0_cond_beta, L1_cond_tau_ctx, L1_cond_Wg, L1_cond_bg, L1_cond_Wn1, L1_cond_bn1, L1_cond_Wsoma, L1_cond_bsoma, L1_cond_Wtemp, L1_cond_btemp, L1_cond_Wout, L1_cond_gamma, L1_cond_beta):
    import jax
    import jax.numpy as jnp

    def _L0_cond_ref(hidden_states, language_ids, W1, b1, W2, b2, gamma, beta):
        import jax, jax.numpy as jnp
        import numpy as np
        LN_EPS = 1e-05
        w1 = W1[language_ids]
        w2 = W2[language_ids]
        h = jnp.einsum('bsh,bha->bsa', hidden_states, w1) + b1[language_ids][:, None, :]
        h = jax.nn.relu(h)
        adapted = jnp.einsum('bsa,bah->bsh', h, w2) + b2[language_ids][:, None, :]
        x = hidden_states + adapted
        mean = jnp.mean(x, axis=-1, keepdims=True)
        var = jnp.mean(jnp.square(x - mean), axis=-1, keepdims=True)
        normed = (x - mean) * jax.lax.rsqrt(var + LN_EPS)
        return normed * gamma[language_ids][:, None, :] + beta[language_ids][:, None, :]

    def _L1_cond_ref(x, tau_ctx, tau_raws, Wg, bg, Wn1, bn1, Wn2, bn2, blend, Wsoma, bsoma, Wtemp, btemp, Wout, gamma, beta):
        import jax, jax.numpy as jnp
        import numpy as np
        import math
        B, T, E, D = (4, 1024, 512, 4)

        def _tau_init(t):
            a = 0.1 ** (1.0 / max(t - 1, 1))
            tt = -math.log(max(a, 1e-10))
            return math.log(math.exp(tt) - 1 + 1e-10)

        def causal_ema(b, tau_raw):
            alpha = jnp.exp(-jax.nn.softplus(tau_raw)).astype(b.dtype)

            def step(h, bt):
                h = alpha * h + bt
                return (h, h)
            h0 = jnp.zeros((b.shape[0], b.shape[2]), b.dtype)
            _, hs = jax.lax.scan(step, h0, jnp.swapaxes(b, 0, 1))
            return jnp.swapaxes(hs, 0, 1)
        ctx = causal_ema(x, tau_ctx)
        gate_in = jnp.concatenate([x, ctx], axis=-1)
        wg = jax.nn.sigmoid(jnp.einsum('btc,ec->bte', gate_in, Wg) + bg)
        gated = x * wg
        h1 = jax.nn.gelu(jnp.einsum('btc,hc->bth', x, Wn1) + bn1, approximate=False)
        mod = 0.5 + jax.nn.sigmoid(jnp.einsum('bth,dh->btd', h1, Wn2) + bn2)
        traces = jax.vmap(lambda tau, m: causal_ema(gated * m[..., None], tau))(tau_raws, jnp.moveaxis(mod, -1, 0))
        blend_w = jax.nn.softmax(blend, axis=0)
        temporal = jnp.einsum('dbtc,dc->btc', traces, blend_w)
        gate = jax.nn.sigmoid(jnp.einsum('btc,ec->bte', temporal, Wtemp) + btemp)
        soma = jax.nn.gelu(jnp.einsum('btc,ec->bte', x, Wsoma) + bsoma, approximate=False)
        out = jnp.einsum('btc,ec->bte', soma * gate, Wout)
        mu = out.mean(-1, keepdims=True)
        var = out.var(-1, keepdims=True)
        return (out - mu) / jnp.sqrt(var + 1e-05) * gamma + beta
    x = x + _L0_cond_ref(x, itok_B_0_8, L0_cond_W1, L0_cond_b1, L0_cond_W2, L0_cond_b2, L0_cond_gamma, L0_cond_beta)
    x = x + _L1_cond_ref(x, L1_cond_tau_ctx, condB_tauraws, L1_cond_Wg, L1_cond_bg, L1_cond_Wn1, L1_cond_bn1, cond_256, condB_bn2, cond_1024, L1_cond_Wsoma, L1_cond_bsoma, L1_cond_Wtemp, L1_cond_btemp, L1_cond_Wout, L1_cond_gamma, L1_cond_beta)
    return x

_drawn_inputs = setup_inputs


def setup_inputs(seed=0):
    import zlib

    import numpy as np

    out = dict(_drawn_inputs(seed))
    spreads = {'condB_bn2': (0.0, 2.0),
     'L0_cond_b1': (0.0, 0.1),
     'L0_cond_b2': (0.0, 0.1),
     'L0_cond_gamma': (1.0, 0.2),
     'L0_cond_beta': (0.0, 0.1),
     'L1_cond_bg': (-0.5, 0.6),
     'L1_cond_bn1': (0.0, 2.0),
     'L1_cond_bsoma': (0.0, 0.1),
     'L1_cond_btemp': (0.0, 0.8),
     'L1_cond_gamma': (1.0, 0.2),
     'L1_cond_beta': (0.0, 0.1)}
    factors = {'condB_tauraws': 8.0, 'cond_256': 8.0, 'cond_1024': 28.323, 'L1_cond_Wn1': 8.0}
    for name, (base, spread) in spreads.items():
        noise = np.random.default_rng([zlib.crc32(name.encode()), seed]).standard_normal(out[name].shape)
        drawn = base * np.exp(spread * noise) if base else spread * noise
        out[name] = jnp.asarray(drawn.astype(out[name].dtype))
    for name, factor in factors.items():
        out[name] = (out[name] * factor).astype(out[name].dtype)
    return out
```

```python
import concourse.bass as bass
from concourse import mybir
from contextlib import ExitStack

P = 128
BATCHES, SEQ, C = 8, 1024, 512
A = 128
D = 8
LANGS = 10
TOK = 512
TILES = BATCHES * SEQ // TOK
NB = TOK // P
NC = C // P
L = 32
NI = P // L
NQ = 4
NH = D // NQ
SPANS = TOK // L
LEVELS = 10
EPS = 1e-5

AT_IDENT = 0
AT_SEL = AT_IDENT + P
AT_DBITS = AT_SEL + NI * P
AT_DMASK = AT_DBITS + 5 * L
AT_QBITS = AT_DMASK + L
AT_QMASK = AT_QBITS + 5 * 32
AT_TBITS = AT_QMASK + 32
AT_RBITS = AT_TBITS + 5 * L
AT_IMASK = AT_RBITS + 5
CONSTS = AT_IMASK + NI

AL_JD, AL_Q, AL_ROW, AL_CTX = 0, 1, 3, 11
ALS = 12


def cond_resid_kernel(nc, x, xc, ids, w1, w2, b1, b2, g0, be0, wg, wn1, wsoma, wtemp, wout, wn2,
                      bg, g1, be1, cols, taus, bn2, blend, blend_jd, consts, out):
    F = mybir.dt.float32
    ALU = mybir.AluOpType
    ACT = mybir.ActivationFunctionType
    AX = mybir.AxisListType

    out_tiles = out.rearrange("b (h t) c -> (b h) t c", t=TOK)

    ctx = ExitStack()
    with ctx:
        def sb(name, shape, dt=F):
            return ctx.enter_context(nc.sbuf_tensor(name, shape, dt))

        def bank(name):
            return ctx.enter_context(nc.psum_tensor(name, [P, 512], F))

        def sem(name):
            return ctx.enter_context(nc.semaphore(name))

        Wg = sb("Wg", [P, 2 * NC, C])
        Wn1 = sb("Wn1", [P, NC, A])
        Wsoma = sb("Wsoma", [P, NC, C])
        Wtemp = sb("Wtemp", [P, NC, C])
        Wout = sb("Wout", [P, NC, C])
        Wn2 = sb("Wn2", [P, D])
        bg_row = sb("bg_row", [P, C])
        gamma1_row = sb("gamma1_row", [P, C])
        beta1_row = sb("beta1_row", [P, C])
        bn2_row = sb("bn2_row", [1, NB * D])
        ones_row = sb("ones_row", [1, P])
        minus_half = sb("minus_half", [P, NB])
        col = sb("col", [P, 9])
        lang = sb("lang", [1, BATCHES], mybir.dt.int32)
        W1 = sb("W1", [P, NC, A])
        W2 = sb("W2", [P, C])
        b1_col = sb("b1_col", [P, 1])
        b2_row = sb("b2_row", [P, C])
        gamma0_row = sb("gamma0_row", [P, C])
        beta0_row = sb("beta0_row", [P, C])
        con = sb("con", [P, CONSTS])
        ident = con[:, AT_IDENT:AT_IDENT + P]
        alpha = sb("alpha", [P, LEVELS, ALS])
        alpha_1 = sb("alpha_1", [P, LEVELS, ALS])
        factor = sb("factor", [P, 32])
        w_qs = sb("w_qs", [P, NH, C])
        w_jd = sb("w_jd", [P, C])
        Dpow = sb("Dpow", [P, NH, L])
        Rpow = sb("Rpow", [P, NI, D])
        Qpow = sb("Qpow", [P, 32])
        Tpow = sb("Tpow", [P, L])
        Epow = sb("Epow", [P, 2 * NB, P])
        x_t = sb("x_t", [P, NB, C])
        xT = sb("xT", [P, NC, TOK])
        h = sb("h", [P, TOK])
        x1 = [sb(f"x1_{n}", [P, NB, C]) for n in range(2)]
        x1T = sb("x1T", [P, NC, TOK])
        ema = sb("ema", [P, NC, TOK])
        ema_last = sb("ema_last", [P, NC])
        h1 = sb("h1", [P, TOK])
        m_nat = sb("m_nat", [P, NB, D])
        m_rep = sb("m_rep", [P, NB * NI, NH])
        Arep = sb("Arep", [P, NB * NI, NH, L])
        Bm = sb("Bm", [P, NB, NI, D])
        g = sb("g", [P, NB, C])
        grep = [sb(f"grep_{n}", [P, NI, C]) for n in range(2)]
        U = [sb(f"U_{n}", [P, NI, C]) for n in range(2)]
        V = [sb(f"V_{n}", [P, C]) for n in range(2)]
        T_sb = [sb(f"T_sb_{n}", [P, C]) for n in range(2)]
        trT = sb("trT", [P, NC, TOK])
        gate = T_sb
        soma = sb("soma", [P, NC, TOK])
        res = sb("res", [P, NB, C])
        stats0 = sb("stats0", [P, NB, 6])
        mv0 = sb("mv0", [P, NB, 2])
        rstd0 = sb("rstd0", [P, NB])
        stats1 = sb("stats1", [P, NB, 6])
        mv1 = sb("mv1", [P, NB, 2])
        rstd1 = sb("rstd1", [P, NB])
        g_dram = nc.dram_tensor("g_spans", [2, P, C], F, kind="Internal").ap()

        bl = [U[n][:, :, :] for n in range(2)]
        bl_max = T_sb[0]
        bl_sum = T_sb[1]
        bl_jd = V[0]

        chan = [bank(f"chan{n}") for n in range(3)]
        tokp = [bank(f"tokp{n}") for n in range(2)]
        Tp = [bank(f"Tp{n}") for n in range(2)]
        smp = bank("smp")

        ld_w = sem("ld_w")
        ld_small = sem("ld_small")
        ld_blend = sem("ld_blend")
        ld_ids = sem("ld_ids")
        ld_x = sem("ld_x")
        ld_xT = sem("ld_xT")
        ld_lang = sem("ld_lang")
        g_stored = sem("g_stored")
        grep_in = [sem(f"grep_in{n}") for n in range(2)]
        stored = sem("stored")
        names = {"h": 1, "temp": 4, "n1": 1, "soma": 4, "trx": 4, "tt": 4,
                 "out": 4, "y": 4, "wg": 4, "m": 1, "mrep": 1, "S": 2, "Uused": 8, "T": 4}
        full = {n: sem(f"{n}_full") for n in names}
        h_ready, gate_ready, h1_ready, soma_ready = sem("h_ready"), sem("gate_ready"), sem("h1_ready"), sem("soma_ready")
        msig_ready, sig_ready, x1T_ready = sem("msig_ready"), sem("sig_ready"), sem("x1T_ready")
        T_ready, trT_ready, out_copied = sem("T_ready"), sem("trT_ready"), sem("out_copied")
        setup_exp = sem("setup_exp")
        setup_step = sem("setup_step")
        tables_ready = sem("tables_ready")
        sg_ready, ln1_step, res_ready = sem("sg_ready"), sem("ln1_step"), sem("res_ready")
        y_ready, ln0_step, x1_ready = sem("y_ready"), sem("ln0_step"), sem("x1_ready")
        m_ready, Bm_ready, mrep_ready, A_ready = sem("m_ready"), sem("Bm_ready"), sem("mrep_ready"), sem("A_ready")
        pre_ready, g_ready, U_ready, V_ready = sem("pre_ready"), sem("g_ready"), sem("U_ready"), sem("V_ready")
        last_kept, ema_ready = sem("last_kept"), sem("ema_ready")
        ones_ready = sem("ones_ready")
        rstd0_ready, rstd1_ready = sem("rstd0_ready"), sem("rstd1_ready")
        xb2_ready, xbeta_ready, x1b_ready = sem("xb2_ready"), sem("xbeta_ready"), sem("x1b_ready")

        def upto(per_tile, tile, j):
            return tile * per_tile + (j + 1)

        def run_slots(eng, slot, last_loop=TILES - 2):
            slot(-1, 1, False, False, True)
            slot(0, 0, False, True, True)
            pairs = last_loop // 2
            with eng.Fori(0, pairs) as r:
                slot(r * 2 + 1, 1, True, True, True)
                slot(r * 2 + 2, 0, True, True, True)
            for k in range(2 * pairs + 1, TILES + 1):
                slot(k, k % 2, True, k < TILES, k + 1 < TILES)

        chan_order = [("h", 1, 0)] + [("temp", -1, e) for e in range(4)] + [("n1", 0, 0)] \
            + [("soma", 0, e) for e in range(4)] + [("trx", 1, b) for b in range(4)] + [("tt", 0, b) for b in range(4)]
        tok_order = [("out", -1, b) for b in range(4)] + [("y", 1, b) for b in range(4)] + [("wg", 0, b) for b in range(4)]
        read_by = {"h": h_ready, "temp": gate_ready, "n1": h1_ready, "soma": soma_ready, "trx": x1T_ready,
                   "tt": trT_ready, "out": out_copied, "y": y_ready, "wg": pre_ready}

        def bank_of(order, banks, name, j):
            at = [n for n, (s, _, i) in enumerate(order) if (s, i) == (name, j)][0]
            return banks[at % len(banks)]

        def wait_bank(pe, order, banks, k, name, j):
            at = [n for n, (s, _, i) in enumerate(order) if (s, i) == (name, j)][0]
            while True:
                at -= len(banks)
                if at < 0:
                    at += len(order)
                    k = k - 1
                s, ahead, i = order[at]
                tile = k + ahead
                if isinstance(k, int):
                    if k < -1:
                        return
                    if not 0 <= tile < TILES:
                        continue
                pe.wait_ge(read_by[s], upto(names[s], tile, i))
                return

        block = ctx.enter_context(nc.Block())

        @block.sync
        def _(sp):
            sp.dma_start(lang[:, :], ids).then_inc(ld_ids, 16)
            sp.dma_start(xT[:, :, :], xc[0].rearrange("(n p) t -> p n t", p=P)).then_inc(ld_xT, 16)
            sp.dma_start(x_t[:, :, :], x[0].rearrange("(n p) c -> p n c", p=P)).then_inc(ld_x, 16)
            sp.wait_ge(ld_ids, 16)

            def load_language(batch):
                one = sp.value_load(lang[0:1, bass.ds(batch, 1)], min_val=0, max_val=LANGS - 1)
                sp.dma_start(W1[:, :, :], w1[bass.ds(one, 1)].rearrange("a (n p) m -> p (a n) m", p=P)).then_inc(ld_lang, 16)
                sp.dma_start(W2[:, :], w2[bass.ds(one, 1)].rearrange("a p m -> p (a m)")).then_inc(ld_lang, 16)
                sp.dma_start(b1_col[:, :], b1[bass.ds(one, 1)].rearrange("a (p m) -> p (a m)", p=P)).then_inc(ld_lang, 16)
                for row, src in ((b2_row, b2), (gamma0_row, g0), (beta0_row, be0)):
                    sp.dma_start(row[:, :], src[bass.ds(one, 1)].to_broadcast([P, C])).then_inc(ld_lang, 16)

            load_language(0)
            sp.dma_start(con[:, :], consts).then_inc(ld_small, 16)
            sp.dma_start(alpha[:, 0, :], taus).then_inc(ld_small, 16)
            sp.dma_start(col[:, :], cols).then_inc(ld_small, 16)
            sp.dma_start(bn2_row[:, :], bn2).then_inc(ld_small, 16)
            for n in range(2):
                sp.dma_start(bl[n], blend[4 * n:4 * n + 4].unsqueeze(0).to_broadcast([P, 4, C])).then_inc(ld_blend, 16)
            sp.dma_start(bl_jd[:, :], blend_jd).then_inc(ld_blend, 16)
            for dst, src in ((Wn1, wn1), (Wsoma, wsoma), (Wg, wg), (Wtemp, wtemp), (Wout, wout)):
                sp.dma_start(dst[:, :, :], src.rearrange("(n p) m -> p n m", p=P)).then_inc(ld_w, 16)
            sp.dma_start(Wn2[:, :], wn2).then_inc(ld_w, 16)
            for row, src in ((bg_row, bg), (gamma1_row, g1), (beta1_row, be1)):
                sp.dma_start(row[:, :], src.to_broadcast([P, C])).then_inc(ld_w, 16)

            def slot(k, odd, has_prev, has_cur, has_next):
                ahead = not isinstance(k, int) or k + 2 < TILES
                if ahead:
                    sp.wait_ge(full["h"], upto(1, k + 1, 0))
                    sp.dma_start(xT[:, :, :], xc[bass.ds(k + 2, 1)].rearrange("a (n p) t -> p (a n) t", p=P)).then_inc(ld_xT, 16)
                if has_prev:
                    for b in range(NB):
                        sp.wait_ge(res_ready, upto(4, k - 1, b))
                        sp.dma_start(out_tiles[bass.ds(k - 1, 1), b * P:(b + 1) * P, :].rearrange("a p c -> p (a c)"),
                                     res[:, b, :]).then_inc(stored, 16)
                if ahead:
                    sp.wait_ge(x1_ready, upto(4, k + 1, NB - 1))
                    sp.dma_start(x_t[:, :, :], x[bass.ds(k + 2, 1)].rearrange("a (n p) c -> p (a n) c", p=P)).then_inc(ld_x, 16)
                    if not odd:
                        load_language(k // 2 + 1 if isinstance(k, int) else half(k) + 1)
                if has_cur:
                    for b in range(NB):
                        sp.wait_ge(g_ready, upto(4, k, b))
                        sp.dma_start(g_dram[b % 2], g[:, b, :]).then_inc(g_stored, 16)
                        sp.wait_ge(g_stored, 16 * upto(4, k, b))
                        for q in range(NQ):
                            sp.dma_start(grep[b % 2][q * L:(q + 1) * L, :, :],
                                         g_dram[b % 2].rearrange("(i s) c -> s i c", s=L)).then_inc(grep_in[b % 2], 16)

            halves = {}

            def half(k):
                return halves["r"] + 1

            slot(-1, 1, False, False, True)
            slot(0, 0, False, True, True)
            pairs = (TILES - 4) // 2
            with sp.Fori(0, pairs) as r:
                halves["r"] = r
                slot(r * 2 + 1, 1, True, True, True)
                slot(r * 2 + 2, 0, True, True, True)
            for k in range(2 * pairs + 1, TILES + 1):
                slot(k, k % 2, True, k < TILES, k + 1 < TILES)
            sp.wait_ge(stored, 16 * NB * TILES)

        @block.gpsimd
        def _(pool):
            nc.gpsimd.memset(ones_row[:, :], 1.0).then_inc(ones_ready, 1)
            nc.gpsimd.memset(minus_half[:, :], -0.5).then_inc(ones_ready, 1)
            pool.wait_ge(ones_ready, 2)
            pool.wait_ge(ld_w, 16 * 9)

            def slot(k, odd, has_prev, has_cur, has_next):
                if has_next:
                    pool.wait_ge(ld_x, 16 * upto(1, k + 1, 0))
                    if odd:
                        pool.wait_ge(ld_lang, 96 * (half_of(k) + 1))
                    for b in range(NB):
                        if has_prev:
                            pool.wait_ge(g_ready, upto(4, k - 1, b))
                            pool.wait_ge(x1b_ready, upto(4, k - 1, b))
                        nc.gpsimd.tensor_tensor(x1[odd ^ 1][:, b, :], x_t[:, b, :], b2_row[:, :], ALU.add).then_inc(xb2_ready, 1)
                        pool.wait_ge(xb2_ready, upto(4, k + 1, b))
                        nc.gpsimd.tensor_tensor(x_t[:, b, :], x_t[:, b, :], beta0_row[:, :], ALU.add).then_inc(xbeta_ready, 1)
                if has_prev:
                    pool.wait_ge(ln1_step, upto(13, k - 1, 8))
                    nc.gpsimd.tensor_tensor(rstd1[:, :], rstd1[:, :], minus_half[:, :], ALU.pow).then_inc(rstd1_ready, 1)
                if has_next:
                    pool.wait_ge(ln0_step, upto(13, k + 1, 8))
                    nc.gpsimd.tensor_tensor(rstd0[:, :], rstd0[:, :], minus_half[:, :], ALU.pow).then_inc(rstd0_ready, 1)
                if has_cur:
                    for b in range(NB):
                        if b == 0 and not (isinstance(k, int) and k == 0):
                            pool.wait_ge(stored, 16 * upto(4, k - 1, NB - 1))
                        pool.wait_ge(x1_ready, upto(4, k, b))
                        nc.gpsimd.tensor_tensor(res[:, b, :], x1[odd][:, b, :], beta1_row[:, :], ALU.add).then_inc(x1b_ready, 1)

            reg = {}

            def half_of(k):
                return (k + 1) // 2 if isinstance(k, int) else reg["r"] + 1

            slot(-1, 1, False, False, True)
            slot(0, 0, False, True, True)
            pairs = (TILES - 2) // 2
            with pool.Fori(0, pairs) as r:
                reg["r"] = r
                slot(r * 2 + 1, 1, True, True, True)
                slot(r * 2 + 2, 0, True, True, True)
            for k in range(2 * pairs + 1, TILES + 1):
                slot(k, k % 2, True, k < TILES, k + 1 < TILES)

        @block.scalar
        def _(act):
            act.wait_ge(ld_small, 64)
            nc.scalar.activation(alpha[:, 0, :], alpha[:, 0, :], ACT.Exp).then_inc(setup_exp, 1)
            act.wait_ge(setup_step, 4)
            for n in range(2):
                nc.scalar.activation(bl[n], bl[n], ACT.Exp).then_inc(setup_exp, 1)
            nc.scalar.activation(bl_jd[:, :], bl_jd[:, :], ACT.Exp).then_inc(setup_exp, 1)

            def slot(k, odd, has_prev, has_cur, has_next):
                if has_next:
                    act.wait_ge(full["h"], upto(1, k + 1, 0))
                    if not (isinstance(k, int) and k == -1):
                        act.wait_ge(full["y"], upto(4, k, NB - 1))
                    nc.scalar.activation(h[:, :], bank_of(chan_order, chan, "h", 0)[:, :], ACT.Relu,
                                         bias=b1_col[:, :]).then_inc(h_ready, 1)
                if has_prev:
                    for e in range(NC):
                        act.wait_ge(full["temp"], upto(4, k - 1, e))
                        if e >= 2:
                            act.wait_ge(sg_ready, upto(4, k - 1, e - 2))
                        nc.scalar.activation(gate[e % 2][:, :], bank_of(chan_order, chan, "temp", e)[:, :], ACT.Sigmoid,
                                             bias=col[:, 5 + e:6 + e]).then_inc(gate_ready, 1)
                if has_cur:
                    act.wait_ge(full["n1"], upto(1, k, 0))
                    nc.scalar.activation(h1[:, :], bank_of(chan_order, chan, "n1", 0)[:, :], ACT.Gelu,
                                         bias=col[:, 0:1]).then_inc(h1_ready, 1)
                if has_prev:
                    for b in range(NB):
                        act.wait_ge(full["out"], upto(4, k - 1, b))
                        nc.scalar.activation(trT[:, b, :], bank_of(tok_order, tokp, "out", b)[:, :],
                                             ACT.Identity).then_inc(out_copied, 1)
                if has_cur:
                    for e in range(NC):
                        act.wait_ge(full["soma"], upto(4, k, e))
                        nc.scalar.activation(soma[:, e, :], bank_of(chan_order, chan, "soma", e)[:, :], ACT.Gelu,
                                             bias=col[:, 1 + e:2 + e]).then_inc(soma_ready, 1)
                    act.wait_ge(full["m"], upto(1, k, 0))
                    nc.scalar.activation(m_nat[:, :, :], smp[:, 0:NB * D].rearrange("p (b d) -> p b d", b=NB),
                                         ACT.Sigmoid).then_inc(msig_ready, 1)

                def open_gate(b):
                    act.wait_ge(pre_ready, upto(4, k, b))
                    nc.scalar.activation(g[:, b, :], g[:, b, :], ACT.Sigmoid).then_inc(sig_ready, 1)

                def trace(b):
                    act.wait_ge(full["T"], upto(4, k, b))
                    nc.scalar.activation(T_sb[b % 2][:, :], Tp[b % 2][:, :], ACT.Identity).then_inc(T_ready, 1)

                def trace_by_channels(b):
                    act.wait_ge(full["tt"], upto(4, k, b))
                    if has_prev and b == 0:
                        act.wait_ge(res_ready, upto(4, k - 1, NB - 1))
                    nc.scalar.activation(trT[:, :, b * P:(b + 1) * P],
                                         bank_of(chan_order, chan, "tt", b)[:, :].rearrange("p (n t) -> p n t", n=NC),
                                         ACT.Identity).then_inc(trT_ready, 1)

                if has_cur:
                    for b in range(3):
                        open_gate(b)
                    trace(0)
                    open_gate(3)
                    trace(1)
                if has_next:
                    for b in range(NB):
                        act.wait_ge(full["trx"], upto(4, k + 1, b))
                        if has_cur and b == 0:
                            act.wait_ge(full["wg"], upto(4, k, NB - 1))
                        nc.scalar.activation(x1T[:, :, b * P:(b + 1) * P],
                                             bank_of(chan_order, chan, "trx", b)[:, :].rearrange("p (n t) -> p n t", n=NC),
                                             ACT.Identity).then_inc(x1T_ready, 1)
                if has_cur:
                    trace_by_channels(0)
                    trace(2)
                    trace_by_channels(1)
                    trace(3)
                    trace_by_channels(2)
                    trace_by_channels(3)

            run_slots(act, slot)

        @block.vector
        def _(dve):
            steps = [0]

            def link(ins):
                steps[0] += 1
                ins.then_inc(setup_step, 1)
                dve.wait_ge(setup_step, steps[0])

            V_ = nc.vector
            dve.wait_ge(ld_blend, 48)
            link(V_.tensor_reduce(bl_max[:, :], bl[0].rearrange("p d c -> p c d"), AX.X, ALU.max))
            link(V_.tensor_reduce(bl_sum[:, :], bl[1].rearrange("p d c -> p c d"), AX.X, ALU.max))
            link(V_.tensor_tensor(bl_max[:, :], bl_max[:, :], bl_sum[:, :], ALU.max))
            for n in range(2):
                V_.tensor_tensor(bl[n], bl[n], bl_max[:, :].unsqueeze(1).to_broadcast([P, 4, C]), ALU.subtract)
            link(V_.tensor_tensor(bl_jd[:, :], bl_jd[:, :], bl_max[:, :], ALU.subtract))
            dve.wait_ge(setup_exp, 4)
            link(V_.tensor_reduce(bl_max[:, :], bl[0].rearrange("p d c -> p c d"), AX.X, ALU.add))
            link(V_.tensor_reduce(bl_sum[:, :], bl[1].rearrange("p d c -> p c d"), AX.X, ALU.add))
            link(V_.tensor_tensor(bl_sum[:, :], bl_max[:, :], bl_sum[:, :], ALU.add))
            link(V_.reciprocal(bl_sum[:, :], bl_sum[:, :]))
            for hh in range(NH):
                for q in range(NQ):
                    rows = slice(q * L, (q + 1) * L)
                    V_.tensor_tensor(w_qs[rows, hh, :], bl[hh][rows, q, :], bl_sum[rows, :], ALU.mult)
            V_.tensor_tensor(w_jd[:, :], bl_jd[:, :], bl_sum[:, :], ALU.mult)

            link(V_.tensor_scalar(alpha[:, 0, :], alpha[:, 0, :], 1.0, None, ALU.add))
            link(V_.reciprocal(alpha[:, 0, :], alpha[:, 0, :]))
            for n in range(1, LEVELS):
                link(V_.tensor_tensor(alpha[:, n, :], alpha[:, n - 1, :], alpha[:, n - 1, :], ALU.mult))
            link(V_.tensor_scalar(alpha_1[:, :, :], alpha[:, :, :], 1.0, None, ALU.subtract))

            def power(dst, at, level, column):
                for n in range(5):
                    bits = con[:, at + 32 * n:at + 32 * (n + 1)]
                    a = alpha_1[:, level + n, column:column + 1]
                    link(V_.tensor_scalar(dst if n == 0 else factor[:, :], bits, a, 1.0, ALU.mult, ALU.add))
                    if n:
                        link(V_.tensor_tensor(dst, dst, factor[:, :], ALU.mult))

            for hh in range(NH):
                power(Dpow[:, hh, :], AT_DBITS, 0, AL_Q + hh)
                link(V_.tensor_tensor(Dpow[:, hh, :], Dpow[:, hh, :], con[:, AT_DMASK:AT_DMASK + L], ALU.mult))
            power(Qpow[:, :], AT_QBITS, 5, AL_JD)
            link(V_.tensor_tensor(Qpow[:, :], Qpow[:, :], con[:, AT_QMASK:AT_QMASK + 32], ALU.mult))
            power(Tpow[:, :], AT_TBITS, 0, AL_JD)
            link(V_.tensor_scalar(Tpow[:, :], Tpow[:, :], alpha[:, 0, AL_JD:AL_JD + 1], None, ALU.mult))
            E_v = Epow[:, :, :].rearrange("p x (i t) -> p (x i) t", t=L)
            V_.tensor_tensor(E_v, Qpow[:, :].unsqueeze(2).to_broadcast([P, 32, L]),
                             Tpow[:, :].unsqueeze(1).to_broadcast([P, 32, L]), ALU.mult)
            for n in range(5):
                bit = con[:, AT_RBITS + n:AT_RBITS + n + 1]
                f = factor[:, 0:D] if n else factor[:, D:2 * D]
                link(V_.tensor_scalar(f, alpha_1[:, n, AL_ROW:AL_ROW + D], bit, 1.0, ALU.mult, ALU.add))
                if n:
                    link(V_.tensor_tensor(factor[:, D:2 * D], factor[:, D:2 * D], factor[:, 0:D], ALU.mult))
            V_.tensor_tensor(Rpow[:, :, :], factor[:, D:2 * D].unsqueeze(1).to_broadcast([P, NI, D]),
                             con[:, AT_IMASK:AT_IMASK + NI].unsqueeze(2).to_broadcast([P, NI, D]),
                             ALU.mult).then_inc(tables_ready, 1)
            dve.wait_ge(tables_ready, 1)

            def slot(k, odd, has_prev, has_cur, has_next):
                if has_prev:
                    for e in range(NC):
                        dve.wait_ge(gate_ready, upto(4, k - 1, e))
                        V_.tensor_tensor(soma[:, e, :], soma[:, e, :], gate[e % 2][:, :], ALU.mult).then_inc(sg_ready, 1)
                    for b in range(NB):
                        dve.wait_ge(out_copied, upto(4, k - 1, b))
                        V_.bn_stats(stats1[:, b, :], trT[:, b, :]).then_inc(ln1_step, 1)
                if has_next:
                    new = x1[odd ^ 1]
                    for b in range(NB):
                        dve.wait_ge(full["y"], upto(4, k + 1, b))
                        if b == NB - 1 and has_prev:
                            dve.wait_ge(ln1_step, upto(13, k - 1, NB - 1))
                        dve.wait_ge(xb2_ready, upto(4, k + 1, b))
                        V_.tensor_tensor(new[:, b, :], bank_of(tok_order, tokp, "y", b)[:, :], new[:, b, :],
                                         ALU.add).then_inc(y_ready, 1)
                if has_prev:
                    for b in range(NB):
                        if isinstance(k, int):
                            dve.wait_ge(ln1_step, upto(13, k - 1, b))
                        V_.bn_aggr(mv1[:, b, :], stats1[:, b, :]).then_inc(ln1_step, 1)
                    dve.wait_ge(ln1_step, upto(13, k - 1, 7))
                    V_.tensor_scalar(rstd1[:, :], mv1[:, :, 1], EPS, None, ALU.add).then_inc(ln1_step, 1)
                if has_next:
                    for b in range(NB):
                        dve.wait_ge(y_ready, upto(4, k + 1, b))
                        V_.bn_stats(stats0[:, b, :], new[:, b, :]).then_inc(ln0_step, 1)
                if has_prev:
                    for b in range(NB):
                        if b == 0:
                            dve.wait_ge(ln1_step, upto(13, k - 1, 2 * NB - 1))
                        if b == NB - 1 and has_next:
                            dve.wait_ge(ln0_step, upto(13, k + 1, NB - 1))
                        V_.scalar_tensor_tensor(trT[:, b, :], trT[:, b, :], mv1[:, b, 0:1], gamma1_row[:, :],
                                                ALU.subtract, ALU.mult).then_inc(ln1_step, 1)
                if has_next:
                    for b in range(NB):
                        if isinstance(k, int):
                            dve.wait_ge(ln0_step, upto(13, k + 1, b))
                        V_.bn_aggr(mv0[:, b, :], stats0[:, b, :]).then_inc(ln0_step, 1)
                    dve.wait_ge(ln0_step, upto(13, k + 1, 7))
                    V_.tensor_scalar(rstd0[:, :], mv0[:, :, 1], EPS, None, ALU.add).then_inc(ln0_step, 1)
                if has_prev:
                    dve.wait_ge(rstd1_ready, upto(1, k - 1, 0))
                    for b in range(NB):
                        dve.wait_ge(ln1_step, upto(13, k - 1, 9 + b))
                        dve.wait_ge(x1b_ready, upto(4, k - 1, b))
                        V_.scalar_tensor_tensor(res[:, b, :], trT[:, b, :], rstd1[:, b:b + 1], res[:, b, :],
                                                ALU.mult, ALU.add).then_inc(res_ready, 1)
                if has_next:
                    for b in range(NB):
                        V_.scalar_tensor_tensor(new[:, b, :], new[:, b, :], mv0[:, b, 0:1], gamma0_row[:, :],
                                                ALU.subtract, ALU.mult).then_inc(ln0_step, 1)
                    dve.wait_ge(rstd0_ready, upto(1, k + 1, 0))
                    for b in range(NB):
                        dve.wait_ge(ln0_step, upto(13, k + 1, 9 + b))
                        dve.wait_ge(xbeta_ready, upto(4, k + 1, b))
                        V_.scalar_tensor_tensor(new[:, b, :], new[:, b, :], rstd0[:, b:b + 1], x_t[:, b, :],
                                                ALU.mult, ALU.add).then_inc(x1_ready, 1)
                if has_cur:
                    dve.wait_ge(msig_ready, upto(1, k, 0))
                    V_.tensor_scalar(m_nat[:, :, :], m_nat[:, :, :], 0.5, None, ALU.add).then_inc(m_ready, 1)
                    dve.wait_ge(m_ready, upto(1, k, 0))
                    V_.tensor_tensor(Bm[:, :, :, :], m_nat[:, :, :].unsqueeze(2).to_broadcast([P, NB, NI, D]),
                                     Rpow[:, :, :].unsqueeze(1).to_broadcast([P, NB, NI, D]), ALU.mult).then_inc(Bm_ready, 1)

                    def products(b, hh):
                        if hh == 0:
                            dve.wait_ge(grep_in[b % 2], 64 * upto(2, k, b // 2))
                        n = 2 * b + hh
                        if not (isinstance(k, int) and k == 0 and n < 2):
                            dve.wait_ge(full["Uused"], upto(8, k, n - 2))
                        V_.tensor_tensor(U[hh][:, :, :], grep[b % 2][:, :, :],
                                         w_qs[:, hh, :].unsqueeze(1).to_broadcast([P, NI, C]), ALU.mult).then_inc(U_ready, 1)

                    def gate_logits(b):
                        dve.wait_ge(full["wg"], upto(4, k, b))
                        V_.tensor_tensor(g[:, b, :], bank_of(tok_order, tokp, "wg", b)[:, :], bg_row[:, :],
                                         ALU.add).then_inc(pre_ready, 1)

                    def gated(b):
                        dve.wait_ge(sig_ready, upto(4, k, b))
                        V_.tensor_tensor(g[:, b, :], g[:, b, :], x1[odd][:, b, :], ALU.mult).then_inc(g_ready, 1)

                    def span_states(half):
                        rows = slice(half * 64, half * 64 + 64)
                        dve.wait_ge(full["S"], upto(2, k, half))
                        V_.tensor_tensor(V[odd][rows, :], smp[rows, :], w_jd[rows, :], ALU.mult).then_inc(V_ready, 1)

                    gate_logits(0)
                    dve.wait_ge(full["mrep"], upto(1, k, 0))
                    for q in range(NQ):
                        rows = slice(q * L, (q + 1) * L)
                        src = smp[rows, 32:32 + NI * NB * D].rearrange("p (i b h q) -> p b i h q", i=NI, b=NB, h=NH)
                        V_.tensor_copy(m_rep[rows, :, :].rearrange("p (b i) h -> p b i h", b=NB),
                                       src[:, :, :, :, q]).then_inc(mrep_ready, 1)
                    gated(0)
                    dve.wait_ge(mrep_ready, upto(4, k, 3))
                    V_.tensor_tensor(Arep[:, :, :, :],
                                     m_rep[:, :, :].unsqueeze(3).to_broadcast([P, NB * NI, NH, L]),
                                     Dpow[:, :, :].unsqueeze(1).to_broadcast([P, NB * NI, NH, L]),
                                     ALU.mult).then_inc(A_ready, 1)
                    gate_logits(1)
                    gated(1)
                    products(0, 0)
                    gate_logits(2)
                    products(0, 1)
                    gated(2)
                    span_states(0)
                    products(1, 0)
                    gate_logits(3)
                    products(1, 1)
                    gated(3)
                    products(2, 0)
                    span_states(1)
                    products(2, 1)
                    products(3, 0)
                    products(3, 1)
                if has_next:
                    if not odd:
                        V_.tensor_copy(ema_last[:, :], ema[:, :, TOK - 1]).then_inc(last_kept, 1)
                        dve.wait_ge(last_kept, k // 2 + 1 if isinstance(k, int) else reg["r"] + 2)
                    for n in range(NC):
                        if n == 0:
                            dve.wait_ge(x1T_ready, upto(4, k + 1, NB - 1))
                        V_.tensor_tensor_scan(ema[:, n, :], alpha[:, 0, AL_CTX:AL_CTX + 1].to_broadcast([P, TOK]),
                                              x1T[:, n, :], 0.0 if odd else ema_last[:, n:n + 1],
                                              ALU.mult, ALU.add).then_inc(ema_ready, 1)

            reg = {}
            slot(-1, 1, False, False, True)
            slot(0, 0, False, True, True)
            pairs = (TILES - 2) // 2
            with dve.Fori(0, pairs) as r:
                reg["r"] = r
                slot(r * 2 + 1, 1, True, True, True)
                slot(r * 2 + 2, 0, True, True, True)
            for k in range(2 * pairs + 1, TILES + 1):
                slot(k, k % 2, True, k < TILES, k + 1 < TILES)

        @block.tensor
        def _(pe):
            def product(dst, lhsT, rhs, steps, signal):
                for n in range(steps):
                    last = nc.tensor.matmul(dst, lhsT(n), rhs(n), start=(n == 0), stop=(n == steps - 1))
                last.then_inc(full[signal], 1)

            reg = {}

            def slot(k, odd, has_prev, has_cur, has_next):
                def chan_bank(name, j):
                    wait_bank(pe, chan_order, chan, k, name, j)
                    return bank_of(chan_order, chan, name, j)

                def tok_bank(name, j):
                    wait_bank(pe, tok_order, tokp, k, name, j)
                    return bank_of(tok_order, tokp, name, j)

                if has_next:
                    pe.wait_ge(ld_xT, 16 * upto(1, k + 1, 0))
                    if odd:
                        pe.wait_ge(ld_lang, 96 * ((k + 1) // 2 + 1 if isinstance(k, int) else reg["r"] + 2))
                    ps = chan_bank("h", 0)
                    product(ps[:, :], lambda n: W1[:, n, :], lambda n: xT[:, n, :], NC, "h")
                if has_prev:
                    for e in range(NC):
                        ps = chan_bank("temp", e)
                        if e == 0:
                            pe.wait_ge(trT_ready, upto(4, k - 1, NB - 1))
                        product(ps[:, :], lambda n: Wtemp[:, n, e * P:(e + 1) * P], lambda n: trT[:, n, :], NC, "temp")
                if has_cur:
                    ps = chan_bank("n1", 0)
                    pe.wait_ge(x1T_ready, upto(4, k, NB - 1))
                    product(ps[:, :], lambda n: Wn1[:, n, :], lambda n: x1T[:, n, :], NC, "n1")
                if has_prev:
                    pe.wait_ge(sg_ready, upto(4, k - 1, NC - 1))
                    for b in range(NB):
                        ps = tok_bank("out", b)
                        product(ps[:, :], lambda n: soma[:, n, b * P:(b + 1) * P], lambda n: Wout[:, n, :], NC, "out")
                if has_next:
                    pe.wait_ge(h_ready, upto(1, k + 1, 0))
                    for b in range(NB):
                        ps = tok_bank("y", b)
                        product(ps[:, :], lambda n: h[:, b * P:(b + 1) * P], lambda n: W2[:, :], 1, "y")
                if has_cur:
                    for e in range(NC):
                        ps = chan_bank("soma", e)
                        product(ps[:, :], lambda n: Wsoma[:, n, e * P:(e + 1) * P], lambda n: x1T[:, n, :], NC, "soma")
                    pe.wait_ge(h1_ready, upto(1, k, 0))
                    if not (isinstance(k, int) and k == 0):
                        pe.wait_ge(V_ready, upto(2, k - 1, 1))
                    nc.tensor.matmul(smp[:, 0:NB * D], ones_row[:, :], bn2_row[:, :], start=True, stop=False)
                    for b in range(NB):
                        last = nc.tensor.matmul(smp[:, b * D:(b + 1) * D], h1[:, b * P:(b + 1) * P], Wn2[:, :],
                                                start=False, stop=(b == NB - 1))
                    last.then_inc(full["m"], 1)
                    pe.wait_ge(ema_ready, upto(4, k, NC - 1))

                def value_gate(b):
                    ps = tok_bank("wg", b)
                    product(ps[:, :], lambda n: (x1T if n < NC else ema)[:, n % NC, b * P:(b + 1) * P],
                            lambda n: Wg[:, n, :], 2 * NC, "wg")

                def spread_modulation():
                    pe.wait_ge(m_ready, upto(1, k, 0))
                    for i in range(NI):
                        at = AT_SEL + i * P
                        last = nc.tensor.matmul(smp[:, 32 + 32 * i:64 + 32 * i], con[:, at:at + P],
                                                m_nat[:, :, :].rearrange("p b d -> p (b d)"), start=True, stop=True)
                    last.then_inc(full["mrep"], 1)

                def span_states(half):
                    pe.wait_ge(g_ready, upto(4, k, 2 * half + 1))
                    if half == 0:
                        pe.wait_ge(Bm_ready, upto(1, k, 0))
                        pe.wait_ge(mrep_ready, upto(4, k, NQ - 1))
                    for b in (2 * half, 2 * half + 1):
                        last = nc.tensor.matmul(smp[b * 32:(b + 1) * 32, :], Bm[:, b, :, :].rearrange("p i d -> p (i d)"),
                                                g[:, b, :], start=True, stop=True)
                    last.then_inc(full["S"], 1)

                def trace(b):
                    if b == 0:
                        pe.wait_ge(A_ready, upto(1, k, 0))
                    if not (isinstance(k, int) and k == 0 and b < 2):
                        pe.wait_ge(T_ready, upto(4, k, b - 2))
                    for hh in range(NH):
                        pe.wait_ge(U_ready, upto(8, k, 2 * b + hh))
                        for i in range(NI):
                            last = nc.tensor.matmul(Tp[b % 2][i * L:(i + 1) * L, :], Arep[:, b * NI + i, hh, :],
                                                    U[hh][:, i, :], start=(hh == 0), stop=False)
                        last.then_inc(full["Uused"], 1)
                    pe.wait_ge(V_ready, upto(2, k, b // 2))
                    rows = slice(0, 64 * (b // 2 + 1))
                    if odd:
                        nc.tensor.matmul(Tp[b % 2][:, :], Epow[:, NB + b, :], V[0][:, :], start=False, stop=False)
                    nc.tensor.matmul(Tp[b % 2][:, :], Epow[rows, b, :], V[odd][rows, :],
                                     start=False, stop=True).then_inc(full["T"], 1)

                def trace_by_channels(b):
                    ps = chan_bank("tt", b)
                    pe.wait_ge(T_ready, upto(4, k, b))
                    for n in range(NC):
                        last = nc.tensor.transpose(ps[:, n * P:(n + 1) * P], T_sb[b % 2][:, n * P:(n + 1) * P], ident)
                    last.then_inc(full["tt"], 1)

                if has_cur:
                    value_gate(0)
                    spread_modulation()
                    value_gate(1)
                    value_gate(2)
                    span_states(0)
                    trace(0)
                    value_gate(3)
                    trace(1)
                if has_next:
                    for b in range(NB):
                        ps = chan_bank("trx", b)
                        pe.wait_ge(x1_ready, upto(4, k + 1, b))
                        for n in range(NC):
                            last = nc.tensor.transpose(ps[:, n * P:(n + 1) * P], x1[odd ^ 1][:, b, n * P:(n + 1) * P], ident)
                        last.then_inc(full["trx"], 1)
                if has_cur:
                    span_states(1)
                    trace_by_channels(0)
                    trace(2)
                    trace_by_channels(1)
                    trace(3)
                    trace_by_channels(2)
                    trace_by_channels(3)

            pe.wait_ge(ld_w, 16 * 9)
            pe.wait_ge(ones_ready, 2)
            pe.wait_ge(tables_ready, 1)
            slot(-1, 1, False, False, True)
            slot(0, 0, False, True, True)
            pairs = (TILES - 2) // 2
            with pe.Fori(0, pairs) as r:
                reg["r"] = r
                slot(r * 2 + 1, 1, True, True, True)
                slot(r * 2 + 2, 0, True, True, True)
            for k in range(2 * pairs + 1, TILES + 1):
                slot(k, k % 2, True, k < TILES, k + 1 < TILES)


def shape_constants():
    import numpy as np

    r = np.arange(P)
    con = np.zeros((P, CONSTS), np.float32)
    con[:, AT_IDENT:AT_IDENT + P] = np.eye(P)
    for i in range(NI):
        sel = (r[:, None] // L == i) & (r[:, None] % L == r[None, :] % L)
        con[:, AT_SEL + i * P:AT_SEL + (i + 1) * P] = sel
    t = np.arange(32)

    def bits(at, n):
        n = np.clip(n, 0, 31)
        for k in range(5):
            con[:, at + 32 * k:at + 32 * (k + 1)] = (n >> k) & 1

    d = t[None, :] - (r % L)[:, None]
    bits(AT_DBITS, d)
    con[:, AT_DMASK:AT_DMASK + L] = d >= 0
    n = t[None, :] - (r // D)[:, None] - 1
    bits(AT_QBITS, n)
    con[:, AT_QMASK:AT_QMASK + 32] = n >= 0
    bits(AT_TBITS, np.broadcast_to(t[None, :], (P, 32)))
    for k in range(5):
        con[:, AT_RBITS + k] = ((L - 1 - r % L) >> k) & 1
    con[:, AT_IMASK:AT_IMASK + NI] = (r // L)[:, None] == np.arange(NI)[None, :]
    return con


def kernel(x, itok_B_0_8, condB_tauraws, cond_256, condB_bn2, cond_1024, L0_cond_W1, L0_cond_b1, L0_cond_W2,
           L0_cond_b2, L0_cond_gamma, L0_cond_beta, L1_cond_tau_ctx, L1_cond_Wg, L1_cond_bg, L1_cond_Wn1,
           L1_cond_bn1, L1_cond_Wsoma, L1_cond_bsoma, L1_cond_Wtemp, L1_cond_btemp, L1_cond_Wout,
           L1_cond_gamma, L1_cond_beta):
    import numpy as np
    import concourse.bacc as bacc
    from concourse.bass_utils import run_bass_kernel_spmd

    c = np.ascontiguousarray
    x = np.asarray(x)
    xs = x.reshape(TILES, TOK, C)
    taus = np.asarray(condB_tauraws)
    rows = np.arange(P)
    tau_table = np.concatenate([taus[rows % D][:, None], taus[rows // L][:, None], taus[NQ + rows // L][:, None],
                                np.broadcast_to(taus[None, :], (P, D)),
                                np.broadcast_to(np.asarray(L1_cond_tau_ctx).reshape(1, 1), (P, 1))], axis=1)
    by_chunk = lambda v: np.asarray(v).reshape(NC, P).T
    cols = np.concatenate([np.asarray(L1_cond_bn1)[:, None], by_chunk(L1_cond_bsoma), by_chunk(L1_cond_btemp)], axis=1)
    arrays = {
        "x": c(xs), "xc": c(xs.transpose(0, 2, 1)), "ids": np.asarray(itok_B_0_8).reshape(1, BATCHES),
        "w1": c(L0_cond_W1), "w2": c(L0_cond_W2), "b1": c(L0_cond_b1), "b2": c(L0_cond_b2),
        "g0": c(L0_cond_gamma), "be0": c(L0_cond_beta),
        "wg": c(np.asarray(L1_cond_Wg).T), "wn1": c(np.asarray(L1_cond_Wn1).T), "wsoma": c(np.asarray(L1_cond_Wsoma).T),
        "wtemp": c(np.asarray(L1_cond_Wtemp).T), "wout": c(np.asarray(L1_cond_Wout).T), "wn2": c(np.asarray(cond_256).T),
        "bg": np.asarray(L1_cond_bg).reshape(1, C), "g1": np.asarray(L1_cond_gamma).reshape(1, C),
        "be1": np.asarray(L1_cond_beta).reshape(1, C), "cols": c(cols), "taus": c(tau_table),
        "bn2": c(np.tile(np.asarray(condB_bn2), NB)[None, :]), "blend": c(cond_1024),
        "blend_jd": c(np.tile(np.asarray(cond_1024), (SPANS, 1))), "consts": shape_constants(),
    }
    nc = bacc.Bacc("TRN2", target_bir_lowering=False, num_devices=1)
    args = {n: nc.dram_tensor(f"in_{n}", a.shape, mybir.dt.from_np(a.dtype), kind="ExternalInput").ap()
            for n, a in arrays.items()}
    out = nc.dram_tensor("out", (BATCHES, SEQ, C), mybir.dt.float32, kind="ExternalOutput").ap()
    cond_resid_kernel(nc, out=out, **args)
    r = run_bass_kernel_spmd(nc, [{f"in_{n}": a for n, a in arrays.items()}], core_ids=[0])
    return r.results[0]["out"]
```

```python
import concourse.bass as bass
from concourse import mybir
from contextlib import ExitStack

P = 128
BATCHES, SEQ, C = 8, 1024, 512
A = 128
D = 8
LANGS = 10
TOK = 512
TILES = BATCHES * SEQ // TOK
NB = TOK // P
NC = C // P
L = 32
NI = P // L
NQ = 4
NH = D // NQ
SPANS = TOK // L
LEVELS = 10
EPS = 1e-5
HC = C // 2
PIECES = NB * NH * 2

AT_DBITS = 0
AT_DMASK = AT_DBITS + 5 * L
AT_QBITS = AT_DMASK + L
AT_QMASK = AT_QBITS + 5 * 32
AT_TBITS = AT_QMASK + 32
AT_RBITS = AT_TBITS + 5 * L
AT_IMASK = AT_RBITS + 5
BITS = AT_IMASK + NI

AL_JD, AL_Q, AL_ROW, AL_CTX = 0, 1, 3, 11
ALS = 12


def cond_resid_kernel(nc, x, xc, ids, w1, w2, b1, b2, g0, be0, wg, wn1, wsoma, wtemp, wout, wn2,
                      bg, g1, be1, cols, taus, bn2, blend, eye, bits, out):
    F = mybir.dt.float32
    R = mybir.dt.float32r
    ALU = mybir.AluOpType
    ACT = mybir.ActivationFunctionType
    AX = mybir.AxisListType

    out_tiles = out.rearrange("b (h t) c -> (b h) t c", t=TOK)

    ctx = ExitStack()
    with ctx:
        def sb(name, shape, dt=F):
            return ctx.enter_context(nc.sbuf_tensor(name, shape, dt))

        def bank(name):
            return ctx.enter_context(nc.psum_tensor(name, [P, 512], F))

        def sem(name):
            return ctx.enter_context(nc.semaphore(name))

        Wg = [sb(f"Wg_{p}", [P, 2 * NC, C], R) for p in ("hi", "lo")]
        Wn1 = [sb(f"Wn1_{p}", [P, NC, A], R) for p in ("hi", "lo")]
        Wsoma = [sb(f"Wsoma_{p}", [P, NC, C], R) for p in ("hi", "lo")]
        Wtemp = [sb(f"Wtemp_{p}", [P, NC, C], R) for p in ("hi", "lo")]
        Wout = sb("Wout", [P, NC, C])
        Wn2 = sb("Wn2", [P, D])
        bg_row = sb("bg_row", [P, C])
        gamma1_row = sb("gamma1_row", [P, C])
        beta1_row = sb("beta1_row", [P, C])
        bn2_row = sb("bn2_row", [P, D])
        col = sb("col", [P, 9])
        lang = sb("lang", [1, BATCHES], mybir.dt.int32)
        W1 = sb("W1", [P, NC, A])
        W2 = sb("W2", [P, C])
        b1_col = sb("b1_col", [P, 1])
        b2_row = sb("b2_row", [P, C])
        gamma0_row = sb("gamma0_row", [P, C])
        beta0_row = sb("beta0_row", [P, C])
        ident = sb("ident", [P, P])
        alpha_ctx = sb("alpha_ctx", [P, 1])
        w_qs = sb("w_qs", [P, NH, C])
        w_jd = sb("w_jd", [P, C])
        Dpow = sb("Dpow", [P, NH, L])
        Rpow = sb("Rpow", [P, NI, D])
        Epow = sb("Epow", [P, 2 * NB, P])
        grep = [sb(f"grep_{n}", [P, NI, C]) for n in range(2)]
        x_t = grep[0]
        xT = grep[1]
        x1_back = grep[1]
        hid = sb("hid", [P, TOK])
        x1 = [sb(f"x1_{n}", [P, NB, C]) for n in range(2)]
        x1T = [sb(f"x1T_{p}", [P, NC, TOK], R) for p in ("hi", "lo")]
        seq = [sb(f"seq_{p}", [P, NC, TOK], R) for p in ("hi", "lo")]
        Arep = sb("Arep", [P, NB * NI, NH, L])
        Bm = sb("Bm", [P, NB, NI, D])
        g = sb("g", [P, 2, C])
        U = sb("U", [P, 4, NI, HC])
        res = U[:, 0:2, :, :].rearrange("p n i c -> p (n i c)").rearrange("p (b c) -> p b c", c=C)
        ema = U[:, 2:4, :, :].rearrange("p n i c -> p (n i c)").rearrange("p (n t) -> p n t", t=TOK)
        m_nat = U[:, 3, NI - 1, 0:NB * D].rearrange("p (b d) -> p b d", d=D)
        m_rep = U[:, 3, NI - 1, 64:64 + NB * NI * NH].rearrange("p (x h) -> p x h", h=NH)
        V = [sb(f"V_{n}", [P, C]) for n in range(2)]
        T_sb = [hid, sb("T_sb", [P, C])]
        soma = sb("soma", [P, NC, TOK])
        stats0, stats1 = ([V[n][:, at:at + 6 * NB].rearrange("p (b s) -> p b s", s=6) for n in range(2)]
                          for at in (128, 160))
        mv0 = sb("mv0", [P, NB, 2])
        mv1 = sb("mv1", [P, NB, 2])
        rows4 = sb("rows4", [P, 4, NB])
        rstd0, rstd1, minus_half, ema_last = (rows4[:, n, :] for n in range(4))
        g_dram = nc.dram_tensor("g_spans", [2, P, C], F, kind="Internal").ap()
        x1_dram = nc.dram_tensor("x1_tiles", [2, P, NB * C], F, kind="Internal").ap()

        stage = [soma[:, :, :], res, T_sb[1][:, :].rearrange("p (n m) -> p n m", n=NC)]
        spare = Arep[:, :, :, :].rearrange("p b h t -> p (b h t)")
        con = spare[:, 0:BITS]
        alpha = V[0][:, 0:LEVELS * ALS].rearrange("p (n a) -> p n a", a=ALS)
        alpha_1 = V[0][:, 128:128 + LEVELS * ALS].rearrange("p (n a) -> p n a", a=ALS)
        Qpow, Tpow, factor = V[0][:, 256:288], V[0][:, 288:320], V[0][:, 320:352]
        blend_c = V[1][:, 0:NC * D].rearrange("p (n d) -> p n d", d=D)
        blend_s = V[1][:, 64:64 + NC]
        blend_x = ema.rearrange("p n t -> p (n t)")[:, 0:3 * NC * P].rearrange("p (a n c) -> p a n c", a=3, n=NC)

        chan = [bank(f"chan{n}") for n in range(3)]
        tokp = [bank(f"tokp{n}") for n in range(2)]
        Tp = [bank(f"Tp{n}") for n in range(2)]
        smp = bank("smp")

        ld_split = [sem(f"ld_split{n}") for n in range(5)]
        ld_w = sem("ld_w")
        ld_small = sem("ld_small")
        ld_ids = sem("ld_ids")
        ld_x = sem("ld_x")
        ld_xT = sem("ld_xT")
        ld_back = sem("ld_back")
        ld_lang = sem("ld_lang")
        x1_stored = sem("x1_stored")
        g_stored = sem("g_stored")
        grep_in = [sem(f"grep_in{n}") for n in range(2)]
        stored = sem("stored")
        names = {"h": 1, "temp": 4, "n1": 1, "soma": 4, "trx": 4, "tt": 4, "out": 4, "y": 4, "wg": 4,
                 "m": 1, "mrep": 1, "S": 2, "Uused": PIECES // 2, "T": 4}
        full = {n: sem(f"{n}_full") for n in names}
        blend_spread = sem("blend_spread")
        split_hi = sem("split_hi")
        h_ready, gate_ready, h1_ready, soma_ready = sem("h_ready"), sem("gate_ready"), sem("h1_ready"), sem("soma_ready")
        msig_ready, sig_ready, x1hi_ready = sem("msig_ready"), sem("sig_ready"), sem("x1hi_ready")
        T_ready, thi_ready, out_copied, emahi_ready = sem("T_ready"), sem("thi_ready"), sem("out_copied"), sem("emahi_ready")
        setup_exp = sem("setup_exp")
        split_lo = sem("split_lo")
        setup_step = sem("setup_step")
        blend_ready = sem("blend_ready")
        tables_ready = sem("tables_ready")
        sg_ready, ln1_step, res_ready = sem("sg_ready"), sem("ln1_step"), sem("res_ready")
        y_ready, ln0_step, x1_ready = sem("y_ready"), sem("ln0_step"), sem("x1_ready")
        m_pre, m_ready, Bm_ready, mrep_ready, A_ready = sem("m_pre"), sem("m_ready"), sem("Bm_ready"), sem("mrep_ready"), sem("A_ready")
        pre_ready, g_ready, U_ready, V_ready = sem("pre_ready"), sem("g_ready"), sem("U_ready"), sem("V_ready")
        ema_ready, last_kept, emalo_ready = sem("ema_ready"), sem("last_kept"), sem("emalo_ready")
        x1lo_ready, tlo_ready = sem("x1lo_ready"), sem("tlo_ready")
        half_ready = sem("half_ready")
        rstd0_ready, rstd1_ready = sem("rstd0_ready"), sem("rstd1_ready")
        whole_ready, xb2_ready, xbeta_ready, x1b_ready = sem("whole_ready"), sem("xb2_ready"), sem("xbeta_ready"), sem("x1b_ready")

        def upto(per_tile, tile, j):
            return tile * per_tile + (j + 1)

        def run_slots(eng, slot, first=-1):
            pairs = (TILES - 2) // 2
            for k in range(first, 1):
                slot(k, k & 1, False, k >= 0, True, (k - 1) // 2)
            if first < 1:
                with eng.Fori(0, pairs) as r:
                    slot(r * 2 + 1, 1, True, True, True, r)
                    slot(r * 2 + 2, 0, True, True, True, r)
            for k in range(2 * pairs + 1, TILES + 1):
                slot(k, k & 1, True, k < TILES, k + 1 < TILES, (k - 1) // 2)

        chan_order = [("trx", 0, 0), ("trx", 0, 1), ("trx", 0, 2), ("temp", -1, 0), ("trx", 0, 3), ("temp", -1, 1), ("temp", -1, 2),
                      ("temp", -1, 3), ("h", 1, 0), ("n1", 0, 0), ("soma", 0, 0), ("soma", 0, 1), ("tt", 0, 0),
                      ("soma", 0, 2), ("tt", 0, 1), ("tt", 0, 2), ("soma", 0, 3), ("tt", 0, 3)]
        tok_order = [item for b in range(4) for item in (("out", -1, b), ("y", 1, b))] + [("wg", 0, b) for b in range(4)]
        read_by = {"h": h_ready, "temp": sg_ready, "n1": h1_ready, "soma": soma_ready, "trx": x1lo_ready,
                   "tt": tlo_ready, "out": out_copied, "y": y_ready, "wg": pre_ready}

        def bank_of(order, banks, name, j):
            at = [n for n, (s, _, i) in enumerate(order) if (s, i) == (name, j)][0]
            return banks[at % len(banks)]

        def wait_bank(pe, order, banks, k, name, j):
            at = [n for n, (s, _, i) in enumerate(order) if (s, i) == (name, j)][0]
            while True:
                at -= len(banks)
                if at < 0:
                    at += len(order)
                    k = k - 1
                s, ahead, i = order[at]
                tile = k + ahead
                if isinstance(k, int):
                    if k < -1:
                        return
                    if not 0 <= tile < TILES:
                        continue
                pe.wait_ge(read_by[s], upto(names[s], tile, i))
                return

        block = ctx.enter_context(nc.Block())

        @block.sync
        def _(sp):
            sp.dma_start(lang[:, :], ids).then_inc(ld_ids, 16)
            sp.wait_ge(ld_ids, 16)

            def load_language(batch):
                one = sp.value_load(lang[0:1, bass.ds(batch, 1)], min_val=0, max_val=LANGS - 1)
                sp.dma_start(W1[:, :, :], w1[bass.ds(one, 1)].rearrange("a (n p) m -> p (a n) m", p=P)).then_inc(ld_lang, 16)
                sp.dma_start(W2[:, :], w2[bass.ds(one, 1)].rearrange("a p m -> p (a m)")).then_inc(ld_lang, 16)
                sp.dma_start(b1_col[:, :], b1[bass.ds(one, 1)].rearrange("a (p m) -> p (a m)", p=P)).then_inc(ld_lang, 16)
                for row, src in ((b2_row, b2), (gamma0_row, g0), (beta0_row, be0)):
                    sp.dma_start(row[:, :], src[bass.ds(one, 1)].to_broadcast([P, C])).then_inc(ld_lang, 16)

            def load_split(n, src, dst):
                sp.dma_start(dst, src.rearrange("(n p) m -> p n m", p=P)).then_inc(ld_split[n], 16)

            def first_loads():
                sp.dma_start(alpha[:, 0, :], taus).then_inc(ld_small, 16)
                sp.dma_start(col[:, :], cols).then_inc(ld_small, 16)
                sp.dma_start(bn2_row[:, :], bn2.to_broadcast([P, D])).then_inc(ld_small, 16)
                sp.dma_start(blend_c, blend).then_inc(ld_small, 16)
                sp.dma_start(ident[:, :], eye).then_inc(ld_small, 16)
                sp.dma_start(con, bits).then_inc(ld_small, 16)
                load_split(0, wn1, stage[2])
                load_split(1, wsoma, stage[0])
                load_split(2, wg[0:C], stage[1])
                sp.dma_start(Wn2[:, :], wn2).then_inc(ld_w, 16)
                for row, src in ((bg_row, bg), (gamma1_row, g1), (beta1_row, be1)):
                    sp.dma_start(row[:, :], src.to_broadcast([P, C])).then_inc(ld_w, 16)
                sp.wait_ge(split_lo, 2)
                load_split(3, wg[C:2 * C], stage[0])
                sp.wait_ge(split_lo, 3)
                load_split(4, wtemp, stage[1])
                sp.dma_start(Wout[:, :, :], wout.rearrange("(n p) m -> p n m", p=P)).then_inc(ld_w, 16)

            def slot(k, odd, has_prev, has_cur, has_next, r):
                if has_next:
                    if odd:
                        load_language(r + 1)
                    if has_cur and has_prev:
                        sp.wait_ge(U_ready, upto(PIECES, k - 1, 3 * PIECES // 4 - 1))
                    elif has_cur:
                        sp.wait_ge(x1_ready, upto(4, k, NB - 1))
                    sp.dma_start(x_t[:, :, :], x[bass.ds(k + 1, 1)].rearrange("a (n p) c -> p (a n) c", p=P)).then_inc(ld_x, 16)
                    if has_cur and has_prev:
                        sp.wait_ge(U_ready, upto(PIECES, k - 1, PIECES - 1))
                    sp.dma_start(xT[:, :, :], xc[bass.ds(k + 1, 1)].rearrange("a (n p) t -> p (a n) t", p=P)).then_inc(ld_xT, 16)
                if not has_cur and not has_prev:
                    first_loads()
                if has_prev:
                    if has_next:
                        sp.wait_ge(full["h"], upto(1, k + 1, 0))
                    else:
                        sp.wait_ge(U_ready, upto(PIECES, k - 1, PIECES - 1))
                    sp.dma_start(x1_back[:, :, :].rearrange("p b c -> p (b c)"), x1_dram[odd ^ 1]).then_inc(ld_back, 16)

                def store_result():
                    for b in range(NB):
                        sp.wait_ge(res_ready, upto(4, k - 1, b))
                        sp.dma_start(out_tiles[bass.ds(k - 1, 1), b * P:(b + 1) * P, :].rearrange("a p c -> p (a c)"),
                                     res[:, b, :]).then_inc(stored, 16)

                if has_next and not has_cur:
                    sp.wait_ge(x1_ready, upto(4, k + 1, NB - 1))
                if has_prev and not has_cur:
                    store_result()
                if has_cur:
                    for b in range(NB):
                        if b == 1 and has_prev:
                            store_result()
                        sp.wait_ge(g_ready, upto(4, k, b))
                        sp.dma_start(g_dram[b % 2], g[:, b % 2, :]).then_inc(g_stored, 16)
                        sp.wait_ge(g_stored, 16 * upto(4, k, b))
                        for q in range(NQ):
                            sp.dma_start(grep[b % 2][q * L:(q + 1) * L, :, :],
                                         g_dram[b % 2].rearrange("(i s) c -> s i c", s=L)).then_inc(grep_in[b % 2], 16)
                if has_next:
                    if has_cur:
                        sp.wait_ge(x1_stored, 16 * upto(1, k, 0))
                    sp.dma_start(x1_dram[odd ^ 1], x1[odd ^ 1][:, :, :].rearrange("p b c -> p (b c)")).then_inc(x1_stored, 16)

            run_slots(sp, slot)
            sp.wait_ge(stored, 16 * NB * TILES)
            sp.wait_ge(x1_stored, 16 * TILES)

        @block.gpsimd
        def _(pool):
            nc.gpsimd.memset(minus_half, -0.5).then_inc(half_ready, 1)
            pool.wait_ge(half_ready, 1)

            def slot(k, odd, has_prev, has_cur, has_next, r):
                if has_cur:
                    for n in range(NC):
                        if n == 0:
                            if has_prev:
                                pool.wait_ge(full["Uused"], upto(PIECES // 2, k - 1, PIECES // 2 - 1))
                            pool.wait_ge(x1lo_ready, upto(4, k, NB - 1))
                        if n == 0 and not has_prev:
                            pool.wait_ge(blend_spread, 1)
                        nc.gpsimd.tensor_tensor(ema[:, n, :], x1T[0][:, n, :].bitcast(F), x1T[1][:, n, :].bitcast(F),
                                                ALU.add).then_inc(whole_ready, 1)
                if has_next:
                    pool.wait_ge(ld_x, 16 * upto(1, k + 1, 0))
                    if odd:
                        pool.wait_ge(ld_lang, 96 * (r + 2))
                    for b in range(NB):
                        if has_prev:
                            pool.wait_ge(g_ready, upto(4, k - 1, b))
                            if b == 0:
                                pool.wait_ge(x1_stored, 16 * upto(1, k - 1, 0))
                        nc.gpsimd.tensor_tensor(x1[odd ^ 1][:, b, :], x_t[:, b, :], b2_row[:, :], ALU.add).then_inc(xb2_ready, 1)
                        pool.wait_ge(xb2_ready, upto(4, k + 1, b))
                        nc.gpsimd.tensor_tensor(x_t[:, b, :], x_t[:, b, :], beta0_row[:, :], ALU.add).then_inc(xbeta_ready, 1)
                if has_prev:
                    pool.wait_ge(ld_back, 16 * upto(1, k - 1, 0))
                    if isinstance(k, int):
                        pool.wait_ge(ld_w, 16 * 5)
                    for b in range(NB):
                        nc.gpsimd.tensor_tensor(x1_back[:, b, :], x1_back[:, b, :], beta1_row[:, :], ALU.add).then_inc(x1b_ready, 1)
                    pool.wait_ge(ln1_step, upto(13, k - 1, 8))
                    nc.gpsimd.tensor_tensor(rstd1, rstd1, minus_half, ALU.pow).then_inc(rstd1_ready, 1)
                if has_next:
                    pool.wait_ge(ln0_step, upto(13, k + 1, 8))
                    nc.gpsimd.tensor_tensor(rstd0, rstd0, minus_half, ALU.pow).then_inc(rstd0_ready, 1)

            slot(-1, 1, False, False, True, -1)
            pool.wait_ge(ld_w, 16 * 5)
            run_slots(pool, slot, first=0)

        @block.scalar
        def _(act):
            def split(n, stage_n, dst):
                act.wait_ge(ld_split[n], 16)
                nc.scalar.activation(dst, stage[stage_n], ACT.Identity).then_inc(split_hi, 1)

            def slot(k, odd, has_prev, has_cur, has_next, r):
                def high(name, b, dst, ready):
                    act.wait_ge(full[name], upto(4, k, b))
                    nc.scalar.activation(dst[0][:, :, b * P:(b + 1) * P],
                                         bank_of(chan_order, chan, name, b)[:, :].rearrange("p (n t) -> p n t", n=NC),
                                         ACT.Identity).then_inc(ready, 1)

                def soma_gelu(e):
                    act.wait_ge(full["soma"], upto(4, k, e))
                    nc.scalar.activation(soma[:, e, :], bank_of(chan_order, chan, "soma", e)[:, :], ACT.Gelu,
                                         bias=col[:, 1 + e:2 + e]).then_inc(soma_ready, 1)

                if has_cur:
                    for b in range(3):
                        high("trx", b, x1T, x1hi_ready)
                for e in range(NC):
                    if has_prev:
                        ps = bank_of(chan_order, chan, "temp", e)
                        act.wait_ge(full["temp"], upto(4, k - 1, e))
                        nc.scalar.activation(ps[:, :], ps[:, :], ACT.Sigmoid, bias=col[:, 5 + e:6 + e]).then_inc(gate_ready, 1)
                    if has_cur and e == 0:
                        high("trx", 3, x1T, x1hi_ready)
                if has_next:
                    act.wait_ge(full["h"], upto(1, k + 1, 0))
                    nc.scalar.activation(hid[:, :], bank_of(chan_order, chan, "h", 0)[:, :], ACT.Relu,
                                         bias=b1_col[:, :]).then_inc(h_ready, 1)
                if has_cur:
                    for n in range(NC):
                        act.wait_ge(ema_ready, upto(4, k, n))
                        nc.scalar.activation(seq[0][:, n, :], ema[:, n, :], ACT.Identity).then_inc(emahi_ready, 1)
                if has_prev:
                    for b in range(NB):
                        act.wait_ge(full["out"], upto(4, k - 1, b))
                        nc.scalar.activation(res[:, b, :], bank_of(tok_order, tokp, "out", b)[:, :],
                                             ACT.Identity).then_inc(out_copied, 1)
                if has_cur:
                    act.wait_ge(full["n1"], upto(1, k, 0))
                    nc.scalar.activation(hid[:, :], bank_of(chan_order, chan, "n1", 0)[:, :], ACT.Gelu,
                                         bias=col[:, 0:1]).then_inc(h1_ready, 1)
                    soma_gelu(0)
                    act.wait_ge(m_pre, upto(1, k, 0))
                    nc.scalar.activation(m_nat, m_nat, ACT.Sigmoid).then_inc(msig_ready, 1)

                def open_gate(b):
                    act.wait_ge(pre_ready, upto(4, k, b))
                    nc.scalar.activation(g[:, b % 2, :], g[:, b % 2, :], ACT.Sigmoid).then_inc(sig_ready, 1)

                def trace(b):
                    act.wait_ge(full["T"], upto(4, k, b))
                    nc.scalar.activation(T_sb[b % 2][:, :], Tp[b % 2][:, :], ACT.Identity).then_inc(T_ready, 1)

                if has_cur:
                    for b in range(3):
                        open_gate(b)
                    trace(0)
                    open_gate(3)
                    trace(1)
                    soma_gelu(1)
                    high("tt", 0, seq, thi_ready)
                    trace(2)
                    soma_gelu(2)
                    high("tt", 1, seq, thi_ready)
                    high("tt", 2, seq, thi_ready)
                    trace(3)
                    soma_gelu(3)
                    high("tt", 3, seq, thi_ready)

            act.wait_ge(ld_small, 96)
            nc.scalar.activation(alpha[:, 0, :], alpha[:, 0, :], ACT.Exp).then_inc(setup_exp, 1)
            act.wait_ge(blend_ready, 1)
            nc.scalar.activation(blend_c, blend_c, ACT.Exp).then_inc(setup_exp, 1)
            split(0, 2, Wn1[0][:, :, :])
            slot(-1, 1, False, False, True, -1)
            split(1, 0, Wsoma[0][:, :, :])
            split(2, 1, Wg[0][:, 0:NC, :])
            act.wait_ge(blend_spread, 1)
            for hh in range(NH):
                nc.scalar.activation(w_qs[:, hh, :], Tp[hh][:, :], ACT.Identity)
            nc.scalar.activation(w_jd[:, :], smp[:, :], ACT.Identity).then_inc(setup_exp, 1)
            split(3, 0, Wg[0][:, NC:2 * NC, :])
            split(4, 1, Wtemp[0][:, :, :])
            run_slots(act, slot, first=0)

        @block.vector
        def _(dve):
            steps = [0]

            def link(ins):
                steps[0] += 1
                ins.then_inc(setup_step, 1)
                dve.wait_ge(setup_step, steps[0])

            V_ = nc.vector

            def split(n, stage_n, dst):
                dve.wait_ge(split_hi, n + 1)
                V_.tensor_tensor(dst[1], stage[stage_n], dst[0].bitcast(F), ALU.subtract).then_inc(split_lo, 1)

            def power(dst, at, level, column):
                for n in range(5):
                    bit = con[:, at + 32 * n:at + 32 * (n + 1)]
                    a = alpha_1[:, level + n, column:column + 1]
                    link(V_.tensor_scalar(dst if n == 0 else factor, bit, a, 1.0, ALU.mult, ALU.add))
                    if n:
                        link(V_.tensor_tensor(dst, dst, factor, ALU.mult))

            def small_tables():
                dve.wait_ge(ld_small, 96)
                link(V_.tensor_reduce(blend_s, blend_c, AX.X, ALU.max))
                V_.tensor_tensor(blend_c, blend_c, blend_s.unsqueeze(2).to_broadcast([P, NC, D]), ALU.subtract).then_inc(blend_ready, 1)
                dve.wait_ge(setup_exp, 1)
                link(V_.tensor_scalar(alpha[:, 0, :], alpha[:, 0, :], 1.0, None, ALU.add))
                link(V_.reciprocal(alpha[:, 0, :], alpha[:, 0, :]))
                V_.tensor_copy(alpha_ctx[:, :], alpha[:, 0, AL_CTX:AL_CTX + 1])
                dve.wait_ge(setup_exp, 2)
                link(V_.tensor_reduce(blend_s, blend_c, AX.X, ALU.add))
                link(V_.reciprocal(blend_s, blend_s))
                link(V_.tensor_tensor(blend_c, blend_c, blend_s.unsqueeze(2).to_broadcast([P, NC, D]), ALU.mult))
                for hh in range(NH):
                    for n in range(NC):
                        V_.tensor_copy(blend_x[:, hh, n, :].rearrange("p (q s) -> p q s", q=NQ),
                                       blend_c[:, n, hh * NQ:(hh + 1) * NQ].unsqueeze(2).to_broadcast([P, NQ, L]))
                for n in range(NC):
                    last = V_.tensor_copy(blend_x[:, 2, n, :].rearrange("p (j d) -> p j d", d=D),
                                          blend_c[:, n, :].unsqueeze(1).to_broadcast([P, SPANS, D]))
                last.then_inc(blend_ready, 1)

            def decay_tables():
                for n in range(1, LEVELS):
                    link(V_.tensor_tensor(alpha[:, n, :], alpha[:, n - 1, :], alpha[:, n - 1, :], ALU.mult))
                link(V_.tensor_scalar(alpha_1, alpha, 1.0, None, ALU.subtract))
                for hh in range(NH):
                    power(Dpow[:, hh, :], AT_DBITS, 0, AL_Q + hh)
                    link(V_.tensor_tensor(Dpow[:, hh, :], Dpow[:, hh, :], con[:, AT_DMASK:AT_DMASK + L], ALU.mult))
                power(Qpow, AT_QBITS, 5, AL_JD)
                link(V_.tensor_tensor(Qpow, Qpow, con[:, AT_QMASK:AT_QMASK + 32], ALU.mult))
                power(Tpow, AT_TBITS, 0, AL_JD)
                link(V_.tensor_scalar(Tpow, Tpow, alpha[:, 0, AL_JD:AL_JD + 1], None, ALU.mult))
                V_.tensor_tensor(Epow[:, :, :].rearrange("p x (i t) -> p (x i) t", t=L), Qpow.unsqueeze(2).to_broadcast([P, 32, L]),
                                 Tpow.unsqueeze(1).to_broadcast([P, 32, L]), ALU.mult)
                power_s = factor[:, D:2 * D]
                for n in range(5):
                    bit = con[:, AT_RBITS + n:AT_RBITS + n + 1]
                    link(V_.tensor_scalar(factor[:, 0:D] if n else power_s, alpha_1[:, n, AL_ROW:AL_ROW + D], bit, 1.0, ALU.mult, ALU.add))
                    if n:
                        link(V_.tensor_tensor(power_s, power_s, factor[:, 0:D], ALU.mult))
                V_.tensor_tensor(Rpow[:, :, :], power_s.unsqueeze(1).to_broadcast([P, NI, D]),
                                 con[:, AT_IMASK:AT_IMASK + NI].unsqueeze(2).to_broadcast([P, NI, D]),
                                 ALU.mult).then_inc(tables_ready, 1)
                dve.wait_ge(tables_ready, 1)

            def slot(k, odd, has_prev, has_cur, has_next, r):
                new = x1[odd ^ 1]

                def low(name, b, dst, hi_ready, ready):
                    dve.wait_ge(hi_ready, upto(4, k, b))
                    at = slice(b * P, (b + 1) * P)
                    V_.tensor_tensor(dst[1][:, :, at], bank_of(chan_order, chan, name, b)[:, :].rearrange("p (n t) -> p n t", n=NC),
                                     dst[0][:, :, at].bitcast(F), ALU.subtract).then_inc(ready, 1)

                def context(n):
                    if odd and n == 0:
                        dve.wait_ge(last_kept, upto(1, k - 1, 0))
                    dve.wait_ge(whole_ready, upto(4, k, n))
                    V_.tensor_tensor_scan(ema[:, n, :], alpha_ctx[:, 0:1].to_broadcast([P, TOK]), ema[:, n, :],
                                          ema_last[:, n:n + 1] if odd else 0.0, ALU.mult, ALU.add).then_inc(ema_ready, 1)

                if has_cur:
                    for b in range(3):
                        low("trx", b, x1T, x1hi_ready, x1lo_ready)
                for e in range(NC):
                    if has_prev:
                        dve.wait_ge(gate_ready, upto(4, k - 1, e))
                        V_.tensor_tensor(soma[:, e, :], bank_of(chan_order, chan, "temp", e)[:, :], soma[:, e, :],
                                         ALU.mult).then_inc(sg_ready, 1)
                    if has_cur:
                        if e == 0:
                            low("trx", 3, x1T, x1hi_ready, x1lo_ready)
                        else:
                            context(e - 1)
                if has_cur:
                    context(NC - 1)
                    for n in range(NC):
                        dve.wait_ge(emahi_ready, upto(4, k, n))
                        V_.tensor_tensor(seq[1][:, n, :], ema[:, n, :], seq[0][:, n, :].bitcast(F), ALU.subtract).then_inc(emalo_ready, 1)
                    V_.tensor_copy(ema_last, ema[:, :, TOK - 1]).then_inc(last_kept, 1)

                def input_statistics(b):
                    dve.wait_ge(y_ready, upto(4, k + 1, b))
                    V_.bn_stats(stats0[odd][:, b, :], new[:, b, :]).then_inc(ln0_step, 1)

                for b in range(NB):
                    if has_prev:
                        dve.wait_ge(out_copied, upto(4, k - 1, b))
                        V_.bn_stats(stats1[odd][:, b, :], res[:, b, :]).then_inc(ln1_step, 1)
                    if has_next:
                        dve.wait_ge(full["y"], upto(4, k + 1, b))
                        dve.wait_ge(xb2_ready, upto(4, k + 1, b))
                        V_.tensor_tensor(new[:, b, :], bank_of(tok_order, tokp, "y", b)[:, :], new[:, b, :],
                                         ALU.add).then_inc(y_ready, 1)
                        if b:
                            if b == NB - 1 and has_prev:
                                dve.wait_ge(ln1_step, upto(13, k - 1, NB - 1))
                            input_statistics(b - 1)
                if has_next:
                    input_statistics(NB - 1)
                if has_prev:
                    for b in range(NB):
                        if isinstance(k, int):
                            dve.wait_ge(ln1_step, upto(13, k - 1, b))
                        V_.bn_aggr(mv1[:, b, :], stats1[odd][:, b, :]).then_inc(ln1_step, 1)
                    dve.wait_ge(ln1_step, upto(13, k - 1, 7))
                    V_.tensor_scalar(rstd1, mv1[:, :, 1], EPS, None, ALU.add).then_inc(ln1_step, 1)
                    for b in range(NB):
                        if b == NB - 1 and has_next:
                            dve.wait_ge(ln0_step, upto(13, k + 1, NB - 1))
                        V_.scalar_tensor_tensor(res[:, b, :], res[:, b, :], mv1[:, b, 0:1], gamma1_row[:, :],
                                                ALU.subtract, ALU.mult).then_inc(ln1_step, 1)
                if has_next:
                    for b in range(NB):
                        if isinstance(k, int):
                            dve.wait_ge(ln0_step, upto(13, k + 1, b))
                        V_.bn_aggr(mv0[:, b, :], stats0[odd][:, b, :]).then_inc(ln0_step, 1)
                    dve.wait_ge(ln0_step, upto(13, k + 1, 7))
                    V_.tensor_scalar(rstd0, mv0[:, :, 1], EPS, None, ALU.add).then_inc(ln0_step, 1)
                if has_cur:
                    dve.wait_ge(full["m"], upto(1, k, 0))
                    V_.tensor_tensor(m_nat, smp[:, 0:NB * D].rearrange("p (b d) -> p b d", b=NB),
                                     bn2_row[:, :].unsqueeze(1).to_broadcast([P, NB, D]), ALU.add).then_inc(m_pre, 1)

                def result():
                    dve.wait_ge(rstd1_ready, upto(1, k - 1, 0))
                    for b in range(NB):
                        dve.wait_ge(ln1_step, upto(13, k - 1, 9 + b))
                        dve.wait_ge(x1b_ready, upto(4, k - 1, b))
                        V_.scalar_tensor_tensor(res[:, b, :], res[:, b, :], rstd1[:, b:b + 1], x1_back[:, b, :],
                                                ALU.mult, ALU.add).then_inc(res_ready, 1)

                if has_prev and not has_cur:
                    result()
                if has_cur:
                    dve.wait_ge(msig_ready, upto(1, k, 0))
                    V_.tensor_scalar(m_nat, m_nat, 0.5, None, ALU.add).then_inc(m_ready, 1)
                if has_next:
                    for b in range(NB):
                        V_.scalar_tensor_tensor(new[:, b, :], new[:, b, :], mv0[:, b, 0:1], gamma0_row[:, :],
                                                ALU.subtract, ALU.mult).then_inc(ln0_step, 1)

                def input_normed():
                    dve.wait_ge(rstd0_ready, upto(1, k + 1, 0))
                    for b in range(NB):
                        dve.wait_ge(ln0_step, upto(13, k + 1, 9 + b))
                        dve.wait_ge(xbeta_ready, upto(4, k + 1, b))
                        V_.scalar_tensor_tensor(new[:, b, :], new[:, b, :], rstd0[:, b:b + 1], x_t[:, b, :],
                                                ALU.mult, ALU.add).then_inc(x1_ready, 1)

                if has_next:
                    input_normed()
                if has_cur:
                    dve.wait_ge(m_ready, upto(1, k, 0))
                    V_.tensor_tensor(Bm[:, :, :, :], m_nat.unsqueeze(2).to_broadcast([P, NB, NI, D]),
                                     Rpow[:, :, :].unsqueeze(1).to_broadcast([P, NB, NI, D]), ALU.mult).then_inc(Bm_ready, 1)

                    def products(b, hh):
                        for c in range(2):
                            n = 4 * b + 2 * hh + c
                            if hh == 0 and c == 0:
                                dve.wait_ge(grep_in[b % 2], 64 * upto(2, k, b // 2))
                            if c == 0 and b == 0:
                                if has_prev and hh == 1:
                                    dve.wait_ge(stored, 16 * upto(4, k - 1, NB - 1))
                            elif c == 0:
                                dve.wait_ge(full["Uused"], upto(PIECES // 2, k, n // 2 - 2))
                            at = slice(c * HC, (c + 1) * HC)
                            V_.tensor_tensor(U[:, (n + 2) % 4, :, :], grep[b % 2][:, :, at],
                                             w_qs[:, hh, at].unsqueeze(1).to_broadcast([P, NI, HC]), ALU.mult).then_inc(U_ready, 1)

                    def gate_logits(b):
                        dve.wait_ge(full["wg"], upto(4, k, b))
                        if b == 2:
                            dve.wait_ge(full["S"], upto(2, k, 0))
                        V_.tensor_tensor(g[:, b % 2, :], bank_of(tok_order, tokp, "wg", b)[:, :], bg_row[:, :],
                                         ALU.add).then_inc(pre_ready, 1)

                    def gated(b):
                        dve.wait_ge(sig_ready, upto(4, k, b))
                        V_.tensor_tensor(g[:, b % 2, :], g[:, b % 2, :], x1[odd][:, b, :], ALU.mult).then_inc(g_ready, 1)

                    def span_states(half):
                        rows = slice(half * 64, half * 64 + 64)
                        dve.wait_ge(full["S"], upto(2, k, half))
                        V_.tensor_tensor(V[odd][rows, :], smp[rows, :], w_jd[rows, :], ALU.mult).then_inc(V_ready, 1)

                    gate_logits(0)
                    dve.wait_ge(full["mrep"], upto(1, k, 0))
                    V_.tensor_copy(m_rep.rearrange("p (b i) h -> p b i h", b=NB),
                                   smp[:, 32:32 + NI * NB * NH].rearrange("p (i b h) -> p b i h", i=NI, b=NB)).then_inc(mrep_ready, 1)
                    gated(0)
                    if has_prev:
                        result()
                    dve.wait_ge(mrep_ready, upto(1, k, 0))
                    V_.tensor_tensor(Arep[:, :, :, :],
                                     m_rep.unsqueeze(3).to_broadcast([P, NB * NI, NH, L]),
                                     Dpow[:, :, :].unsqueeze(1).to_broadcast([P, NB * NI, NH, L]),
                                     ALU.mult).then_inc(A_ready, 1)
                    gate_logits(1)
                    gated(1)
                    products(0, 0)
                    gate_logits(2)
                    products(0, 1)
                    gated(2)
                    span_states(0)
                    products(1, 0)
                    products(1, 1)
                    gate_logits(3)
                    gated(3)
                    products(2, 0)
                    span_states(1)
                    products(2, 1)
                    low("tt", 0, seq, thi_ready, tlo_ready)
                    products(3, 0)
                    products(3, 1)
                    low("tt", 1, seq, thi_ready, tlo_ready)
                    low("tt", 2, seq, thi_ready, tlo_ready)
                    low("tt", 3, seq, thi_ready, tlo_ready)

            small_tables()
            split(0, 2, [w[:, :, :] for w in Wn1])
            slot(-1, 1, False, False, True, -1)
            split(1, 0, [w[:, :, :] for w in Wsoma])
            split(2, 1, [w[:, 0:NC, :] for w in Wg])
            split(3, 0, [w[:, NC:2 * NC, :] for w in Wg])
            split(4, 1, [w[:, :, :] for w in Wtemp])
            decay_tables()
            run_slots(dve, slot, first=0)

        @block.tensor
        def _(pe):
            def product(dst, lhsT, rhs, steps, signal):
                for n in range(steps):
                    last = nc.tensor.matmul(dst, lhsT(n), rhs(n), start=(n == 0), stop=(n == steps - 1))
                last.then_inc(full[signal], 1)

            def split_product(dst, lhsT, rhs, steps, first=True, final=True):
                for n in range(steps):
                    for m, (a, b) in enumerate(((0, 0), (0, 1), (1, 0))):
                        last = nc.tensor.matmul(dst, lhsT(a, n), rhs(b, n), start=(first and n == 0 and m == 0),
                                                stop=(final and n == steps - 1 and m == 2))
                return last

            def slot(k, odd, has_prev, has_cur, has_next, r):
                def chan_bank(name, j):
                    wait_bank(pe, chan_order, chan, k, name, j)
                    return bank_of(chan_order, chan, name, j)

                def tok_bank(name, j):
                    wait_bank(pe, tok_order, tokp, k, name, j)
                    return bank_of(tok_order, tokp, name, j)

                def x1_by_channels(b):
                    ps = chan_bank("trx", b)
                    pe.wait_ge(x1_ready, upto(4, k, b))
                    for n in range(NC):
                        last = nc.tensor.transpose(ps[:, n * P:(n + 1) * P], x1[odd][:, b, n * P:(n + 1) * P], ident[:, :])
                    last.then_inc(full["trx"], 1)

                def temporal_gate(e):
                    ps = chan_bank("temp", e)
                    if e == 0:
                        pe.wait_ge(tlo_ready, upto(4, k - 1, NB - 1))
                        if isinstance(k, int):
                            pe.wait_ge(split_lo, 5)
                    at = slice(e * P, (e + 1) * P)
                    split_product(ps[:, :], lambda a, n: Wtemp[a][:, n, at], lambda a, n: seq[a][:, n, :],
                                  NC).then_inc(full["temp"], 1)

                def soma_of(e):
                    ps = chan_bank("soma", e)
                    at = slice(e * P, (e + 1) * P)
                    split_product(ps[:, :], lambda a, n: Wsoma[a][:, n, at], lambda a, n: x1T[a][:, n, :],
                                  NC).then_inc(full["soma"], 1)

                if has_cur:
                    for b in range(3):
                        x1_by_channels(b)
                for e in range(NC):
                    if has_prev:
                        temporal_gate(e)
                    if has_cur and e == 0:
                        x1_by_channels(3)
                if has_next:
                    pe.wait_ge(ld_xT, 16 * upto(1, k + 1, 0))
                    if odd:
                        pe.wait_ge(ld_lang, 96 * (r + 2))
                    ps = chan_bank("h", 0)
                    product(ps[:, :], lambda n: W1[:, n, :], lambda n: xT[:, n, :], NC, "h")
                for b in range(NB):
                    if has_prev:
                        if b == 0:
                            pe.wait_ge(sg_ready, upto(4, k - 1, NC - 1))
                            if isinstance(k, int):
                                pe.wait_ge(ld_w, 16 * 5)
                        ps = tok_bank("out", b)
                        product(ps[:, :], lambda n: soma[:, n, b * P:(b + 1) * P], lambda n: Wout[:, n, :], NC, "out")
                    if has_next:
                        if b == 0:
                            pe.wait_ge(h_ready, upto(1, k + 1, 0))
                        ps = tok_bank("y", b)
                        product(ps[:, :], lambda n: hid[:, b * P:(b + 1) * P], lambda n: W2[:, :], 1, "y")
                if has_cur:
                    ps = chan_bank("n1", 0)
                    pe.wait_ge(x1lo_ready, upto(4, k, NB - 1))
                    split_product(ps[:, :], lambda a, n: Wn1[a][:, n, :], lambda a, n: x1T[a][:, n, :], NC).then_inc(full["n1"], 1)
                    if isinstance(k, int):
                        pe.wait_ge(split_lo, 4)
                    soma_of(0)
                    pe.wait_ge(h1_ready, upto(1, k, 0))
                    if has_prev:
                        pe.wait_ge(V_ready, upto(2, k - 1, 1))
                    else:
                        pe.wait_ge(setup_exp, 3)
                    for b in range(NB):
                        last = nc.tensor.matmul(smp[:, b * D:(b + 1) * D], hid[:, b * P:(b + 1) * P], Wn2[:, :],
                                                start=True, stop=True)
                    last.then_inc(full["m"], 1)
                    pe.wait_ge(emalo_ready, upto(4, k, NC - 1))

                def value_gate(b, part):
                    ps = tok_bank("wg", b) if part == 0 else bank_of(tok_order, tokp, "wg", b)
                    src, at = (x1T, seq)[part], slice(b * P, (b + 1) * P)
                    last = split_product(ps[:, :], lambda a, n: src[a][:, n, at], lambda a, n: Wg[a][:, part * NC + n, :],
                                         NC, first=part == 0, final=part == 1)
                    if part:
                        last.then_inc(full["wg"], 1)

                def spread_modulation():
                    pe.wait_ge(m_ready, upto(1, k, 0))
                    for i in range(NI):
                        for q in range(NQ):
                            last = nc.tensor.matmul(smp[q * L:(q + 1) * L, 32 + 8 * i:40 + 8 * i], ident[:, i * L:(i + 1) * L],
                                                    U[:, 3, NI - 1, q:NB * D:NQ], start=True, stop=True)
                    last.then_inc(full["mrep"], 1)

                def span_states(half):
                    pe.wait_ge(g_ready, upto(4, k, 2 * half + 1))
                    if half == 0:
                        pe.wait_ge(Bm_ready, upto(1, k, 0))
                        pe.wait_ge(mrep_ready, upto(1, k, 0))
                    for b in (2 * half, 2 * half + 1):
                        last = nc.tensor.matmul(smp[b * 32:(b + 1) * 32, :], Bm[:, b, :, :].rearrange("p i d -> p (i d)"),
                                                g[:, b % 2, :], start=True, stop=True)
                    last.then_inc(full["S"], 1)

                def within_spans(b, hh):
                    if b == 0 and hh == 0:
                        pe.wait_ge(A_ready, upto(1, k, 0))
                    if hh == 0:
                        if b >= 2 or has_prev:
                            pe.wait_ge(T_ready, upto(4, k, b - 2))
                        elif b == 0:
                            pe.wait_ge(setup_exp, 3)
                    for c in range(2):
                        n = 4 * b + 2 * hh + c
                        pe.wait_ge(U_ready, upto(PIECES, k, n))
                        at = slice(c * HC, (c + 1) * HC)
                        for i in range(NI):
                            last = nc.tensor.matmul(Tp[b % 2][i * L:(i + 1) * L, at], Arep[:, b * NI + i, hh, :],
                                                    U[:, (n + 2) % 4, i, :], start=(hh == 0 and c == 0), stop=False)
                    last.then_inc(full["Uused"], 1)

                def from_before(b):
                    pe.wait_ge(V_ready, upto(2, k, b // 2))
                    rows = slice(0, 64 * (b // 2 + 1))
                    if odd:
                        nc.tensor.matmul(Tp[b % 2][:, :], Epow[:, NB + b, :], V[0][:, :], start=False, stop=False)
                    nc.tensor.matmul(Tp[b % 2][:, :], Epow[rows, b, :], V[odd][rows, :],
                                     start=False, stop=True).then_inc(full["T"], 1)

                def trace_by_channels(b):
                    ps = chan_bank("tt", b)
                    pe.wait_ge(T_ready, upto(4, k, b))
                    for n in range(NC):
                        last = nc.tensor.transpose(ps[:, n * P:(n + 1) * P], T_sb[b % 2][:, n * P:(n + 1) * P], ident[:, :])
                    last.then_inc(full["tt"], 1)

                if has_cur:
                    value_gate(0, 0)
                    value_gate(0, 1)
                    spread_modulation()
                    value_gate(1, 0)
                    value_gate(1, 1)
                    value_gate(2, 0)
                    span_states(0)
                    value_gate(2, 1)
                    within_spans(0, 0)
                    value_gate(3, 0)
                    within_spans(0, 1)
                    from_before(0)
                    value_gate(3, 1)
                    within_spans(1, 0)
                    within_spans(1, 1)
                    from_before(1)
                    span_states(1)
                    soma_of(1)
                    within_spans(2, 0)
                    trace_by_channels(0)
                    within_spans(2, 1)
                    from_before(2)
                    soma_of(2)
                    trace_by_channels(1)
                    within_spans(3, 0)
                    trace_by_channels(2)
                    within_spans(3, 1)
                    from_before(3)
                    soma_of(3)
                    trace_by_channels(3)

            pe.wait_ge(ld_small, 96)
            slot(-1, 1, False, False, True, -1)
            pe.wait_ge(blend_ready, 2)
            for n in range(NC):
                at = slice(n * P, (n + 1) * P)
                for hh in range(NH):
                    nc.tensor.transpose(Tp[hh][:, at], blend_x[:, hh, n, :], ident[:, :])
                last = nc.tensor.transpose(smp[:, at], blend_x[:, 2, n, :], ident[:, :])
            last.then_inc(blend_spread, 1)
            pe.wait_ge(tables_ready, 1)
            run_slots(pe, slot, first=0)


def shape_constants():
    import numpy as np

    r = np.arange(P)
    con = np.zeros((P, BITS), np.float32)
    t = np.arange(32)

    def bits(at, n):
        n = np.clip(n, 0, 31)
        for k in range(5):
            con[:, at + 32 * k:at + 32 * (k + 1)] = (n >> k) & 1

    d = t[None, :] - (r % L)[:, None]
    bits(AT_DBITS, d)
    con[:, AT_DMASK:AT_DMASK + L] = d >= 0
    n = t[None, :] - (r // D)[:, None] - 1
    bits(AT_QBITS, n)
    con[:, AT_QMASK:AT_QMASK + 32] = n >= 0
    bits(AT_TBITS, np.broadcast_to(t[None, :], (P, 32)))
    for k in range(5):
        con[:, AT_RBITS + k] = ((L - 1 - r % L) >> k) & 1
    con[:, AT_IMASK:AT_IMASK + NI] = (r // L)[:, None] == np.arange(NI)[None, :]
    return con


def kernel(x, itok_B_0_8, condB_tauraws, cond_256, condB_bn2, cond_1024, L0_cond_W1, L0_cond_b1, L0_cond_W2,
           L0_cond_b2, L0_cond_gamma, L0_cond_beta, L1_cond_tau_ctx, L1_cond_Wg, L1_cond_bg, L1_cond_Wn1,
           L1_cond_bn1, L1_cond_Wsoma, L1_cond_bsoma, L1_cond_Wtemp, L1_cond_btemp, L1_cond_Wout,
           L1_cond_gamma, L1_cond_beta):
    import numpy as np
    import concourse.bacc as bacc
    from concourse.bass_utils import run_bass_kernel_spmd

    c = np.ascontiguousarray
    x = np.asarray(x)
    xs = x.reshape(TILES, TOK, C)
    taus = np.asarray(condB_tauraws)
    rows = np.arange(P)
    tau_table = np.concatenate([taus[rows % D][:, None], taus[rows // L][:, None], taus[NQ + rows // L][:, None],
                                np.broadcast_to(taus[None, :], (P, D)),
                                np.broadcast_to(np.asarray(L1_cond_tau_ctx).reshape(1, 1), (P, 1))], axis=1)
    by_chunk = lambda v: np.asarray(v).reshape(NC, P).T
    cols = np.concatenate([np.asarray(L1_cond_bn1)[:, None], by_chunk(L1_cond_bsoma), by_chunk(L1_cond_btemp)], axis=1)
    arrays = {
        "x": c(xs), "xc": c(xs.transpose(0, 2, 1)), "ids": np.asarray(itok_B_0_8).reshape(1, BATCHES),
        "w1": c(L0_cond_W1), "w2": c(L0_cond_W2), "b1": c(L0_cond_b1), "b2": c(L0_cond_b2),
        "g0": c(L0_cond_gamma), "be0": c(L0_cond_beta),
        "wg": c(np.asarray(L1_cond_Wg).T), "wn1": c(np.asarray(L1_cond_Wn1).T), "wsoma": c(np.asarray(L1_cond_Wsoma).T),
        "wtemp": c(np.asarray(L1_cond_Wtemp).T), "wout": c(np.asarray(L1_cond_Wout).T), "wn2": c(np.asarray(cond_256).T),
        "bg": np.asarray(L1_cond_bg).reshape(1, C), "g1": np.asarray(L1_cond_gamma).reshape(1, C),
        "be1": np.asarray(L1_cond_beta).reshape(1, C), "cols": c(cols), "taus": c(tau_table),
        "bn2": np.asarray(condB_bn2).reshape(1, D),
        "blend": c(np.asarray(cond_1024).reshape(D, NC, P).transpose(2, 1, 0)),
        "eye": np.eye(P, dtype=np.float32), "bits": shape_constants(),
    }
    nc = bacc.Bacc("TRN2", target_bir_lowering=False, num_devices=1)
    args = {n: nc.dram_tensor(f"in_{n}", a.shape, mybir.dt.from_np(a.dtype), kind="ExternalInput").ap()
            for n, a in arrays.items()}
    out = nc.dram_tensor("out", (BATCHES, SEQ, C), mybir.dt.float32, kind="ExternalOutput").ap()
    cond_resid_kernel(nc, out=out, **args)
    r = run_bass_kernel_spmd(nc, [{f"in_{n}": a for n, a in arrays.items()}], core_ids=[0])
    return r.results[0]["out"]
```

```python
import concourse.bass as bass
from concourse import mybir
from contextlib import ExitStack

P = 128
BATCHES, SEQ, C = 8, 1024, 512
A = 128
D = 8
LANGS = 10
TOK = 512
TILES = BATCHES * SEQ // TOK
NB = TOK // P
NC = C // P
L = 32
NI = P // L
NQ = 4
NH = D // NQ
SPANS = TOK // L
LEVELS = 10
EPS = 1e-5
HC = C // 2
PIECES = NB * NH * 2

AT_DBITS = 0
AT_DMASK = AT_DBITS + 5 * L
AT_QBITS = AT_DMASK + L
AT_QMASK = AT_QBITS + 5 * 32
AT_TBITS = AT_QMASK + 32
AT_RBITS = AT_TBITS + 5 * L
AT_IMASK = AT_RBITS + 5
AT_EBITS = AT_IMASK + NI
AT_EMASK = AT_EBITS + 5
BITS = AT_EMASK + D

AL_JD, AL_Q, AL_ROW, AL_CTX = 0, 1, 3, 11
ALS = 12


def cond_resid_kernel(nc, x, xc, ids, w1, w2, b1, b2, g0, be0, wg, wn1, wsoma, wtemp, wout, wn2,
                      bg, g1, be1, cols, taus, bn2, blend, eye, bits, out):
    F = mybir.dt.float32
    R = mybir.dt.float32r
    ALU = mybir.AluOpType
    ACT = mybir.ActivationFunctionType
    AX = mybir.AxisListType

    out_tiles = out.rearrange("b (h t) c -> (b h) t c", t=TOK)

    ctx = ExitStack()
    with ctx:
        def sb(name, shape, dt=F):
            return ctx.enter_context(nc.sbuf_tensor(name, shape, dt))

        def bank(name):
            return ctx.enter_context(nc.psum_tensor(name, [P, 512], F))

        def sem(name):
            return ctx.enter_context(nc.semaphore(name))

        Wg = [sb(f"Wg_{p}", [P, 2 * NC, C], R) for p in ("hi", "lo")]
        Wn1 = [sb(f"Wn1_{p}", [P, NC, A], R) for p in ("hi", "lo")]
        Wsoma = [sb(f"Wsoma_{p}", [P, NC, C], R) for p in ("hi", "lo")]
        Wtemp = [sb(f"Wtemp_{p}", [P, NC, C], R) for p in ("hi", "lo")]
        Wout = sb("Wout", [P, NC, C])
        Wn2 = sb("Wn2", [P, D])
        bg_row = sb("bg_row", [P, C])
        gamma1_row = sb("gamma1_row", [P, C])
        beta1_row = sb("beta1_row", [P, C])
        bn2_row = sb("bn2_row", [P, D])
        columns = sb("columns", [P, 11])
        col, alpha_ctx, b1_col = columns[:, 0:9], columns[:, 9:10], columns[:, 10:11]
        lang = sb("lang", [1, BATCHES], mybir.dt.int32)
        W1 = sb("W1", [P, NC, A])
        W2 = sb("W2", [P, C])
        b2_row = sb("b2_row", [P, C])
        gamma0_row = sb("gamma0_row", [P, C])
        beta0_row = sb("beta0_row", [P, C])
        ident = sb("ident", [P, P])
        w_qs = sb("w_qs", [P, NH, C])
        w_jd = sb("w_jd", [P, C])
        Dpow = sb("Dpow", [P, NH, L])
        Rpow = sb("Rpow", [P, NI, D])
        Epow = sb("Epow", [P, 2 * NB, P])
        Eend = sb("Eend", [P, 2 * (L - D) + D])
        grep = [sb(f"grep_{n}", [P, NI, C]) for n in range(2)]
        x_t = grep[0]
        xT = grep[1]
        x1_back = grep[1]
        hid = sb("hid", [P, TOK])
        x1 = [sb(f"x1_{n}", [P, NB, C]) for n in range(2)]
        x1T = [sb(f"x1T_{p}", [P, NC, TOK], R) for p in ("hi", "lo")]
        seq = [sb(f"seq_{p}", [P, NC, TOK], R) for p in ("hi", "lo")]
        Arep = sb("Arep", [P, NB * NI, NH, L])
        Bm = sb("Bm", [P, NB, NI, D])
        g = sb("g", [P, 2, C])
        U = sb("U", [P, 4, NI, HC])
        res = U[:, 0:2, :, :].rearrange("p n i c -> p (n i c)").rearrange("p (b c) -> p b c", c=C)
        ema = U[:, 2:4, :, :].rearrange("p n i c -> p (n i c)").rearrange("p (n t) -> p n t", t=TOK)
        m_nat = U[:, 3, NI - 1, 0:NB * D].rearrange("p (b d) -> p b d", d=D)
        m_rep = U[:, 3, NI - 1, 64:64 + NB * NI * NH].rearrange("p (x h) -> p x h", h=NH)
        V = [sb(f"V_{n}", [P, C]) for n in range(2)]
        T_sb = [hid, sb("T_sb", [P, C])]
        soma = sb("soma", [P, NC, TOK])
        stats0, stats1 = (V[0][:, at:at + 6 * NB].rearrange("p (b s) -> p b s", s=6)
                          for at in (128, 160))
        mv0, mv1 = (V[0][:, at:at + 2 * NB].rearrange("p (b s) -> p b s", s=2) for at in (192, 208))
        rows4 = sb("rows4", [P, 4, NB])
        rstd0, rstd1, minus_half, ema_last = (rows4[:, n, :] for n in range(4))
        g_dram = nc.dram_tensor("g_spans", [2, L, NI * C], F, kind="Internal").ap()
        x1_dram = nc.dram_tensor("x1_tiles", [2, P, NB * C], F, kind="Internal").ap()

        stage = [soma[:, :, :], res, T_sb[1][:, :].rearrange("p (n m) -> p n m", n=NC)]
        spare = Arep[:, :, :, :].rearrange("p b h t -> p (b h t)")
        con = spare[:, 0:BITS]
        alpha = V[0][:, 0:LEVELS * ALS].rearrange("p (n a) -> p n a", a=ALS)
        alpha_1 = V[0][:, 128:128 + LEVELS * ALS].rearrange("p (n a) -> p n a", a=ALS)
        Qpow, Tpow = V[0][:, 256:288], V[0][:, 288:320]
        factors = g[:, :, :].rearrange("p n c -> p (n c)")[:, 0:5 * 4 * L].rearrange("p (n a t) -> p n a t", n=5, a=4)
        factors_s = V[0][:, 320:320 + 5 * D].rearrange("p (n d) -> p n d", n=5)
        factors_e = V[0][:, 384:389]
        blend_c = V[1][:, 0:NC * D].rearrange("p (n d) -> p n d", d=D)
        blend_s = V[1][:, 64:64 + NC]
        blend_x = ema.rearrange("p n t -> p (n t)")[:, 0:3 * NC * P].rearrange("p (a n c) -> p a n c", a=3, n=NC)

        chan = [bank(f"chan{n}") for n in range(3)]
        tokp = [bank(f"tokp{n}") for n in range(2)]
        Tp = [bank(f"Tp{n}") for n in range(2)]
        smp = bank("smp")

        ld_split = [sem(f"ld_split{n}") for n in range(5)]
        ld_rows, ld_wout = sem("ld_rows"), sem("ld_wout")
        ld_small = sem("ld_small")
        ld_ids = sem("ld_ids")
        ld_x = sem("ld_x")
        ld_xT = sem("ld_xT")
        ld_back = sem("ld_back")
        ld_lang = sem("ld_lang")
        x1_stored = sem("x1_stored")
        g_stored = sem("g_stored")
        grep_in = [sem(f"grep_in{n}") for n in range(2)]
        stored = sem("stored")
        names = {"h": 1, "temp": 4, "n1": 1, "soma": 4, "trx": 4, "tt": 4, "out": 4, "y": 4, "wg": 4,
                 "m": 1, "mrep": 1, "S": 2, "Uused": PIECES // 2, "T": 4, "carry": 1}
        full = {n: sem(f"{n}_full") for n in names}
        blend_spread = sem("blend_spread")
        split_hi = sem("split_hi")
        h_ready, gate_ready, h1_ready, soma_ready = sem("h_ready"), sem("gate_ready"), sem("h1_ready"), sem("soma_ready")
        msig_ready, sig_ready, x1hi_ready = sem("msig_ready"), sem("sig_ready"), sem("x1hi_ready")
        T_ready, thi_ready, out_copied, emahi_ready = sem("T_ready"), sem("thi_ready"), sem("out_copied"), sem("emahi_ready")
        scaled_ready, carry_ready = sem("scaled_ready"), sem("carry_ready")
        setup_exp = sem("setup_exp")
        split_lo = [sem(f"split_lo{n}") for n in range(5)]
        setup_step = sem("setup_step")
        blend_ready = sem("blend_ready")
        tables_ready = sem("tables_ready")
        sg_ready, ln1_step = sem("sg_ready"), sem("ln1_step")
        y_ready, ln0_step, x1_ready = sem("y_ready"), sem("ln0_step"), sem("x1_ready")
        m_pre, m_ready, Bm_ready, mrep_ready, A_ready = sem("m_pre"), sem("m_ready"), sem("Bm_ready"), sem("mrep_ready"), sem("A_ready")
        pre_ready, g_ready, U_ready, V_ready = sem("pre_ready"), sem("g_ready"), sem("U_ready"), sem("V_ready")
        ema_ready, last_kept, emalo_ready = sem("ema_ready"), sem("last_kept"), sem("emalo_ready")
        x1lo_ready, tlo_ready = sem("x1lo_ready"), sem("tlo_ready")
        half_ready = sem("half_ready")
        rstd0_ready, rstd1_ready = sem("rstd0_ready"), sem("rstd1_ready")
        res_ready = sem("res_ready")
        whole_ready, xb2_ready, xbeta_ready, x1b_ready = sem("whole_ready"), sem("xb2_ready"), sem("xbeta_ready"), sem("x1b_ready")

        def upto(per_tile, tile, j):
            return tile * per_tile + (j + 1)

        def run_slots(eng, slot, first=-1):
            pairs = (TILES - 2) // 2
            for k in range(first, 1):
                slot(k, k & 1, False, k >= 0, True, (k - 1) // 2)
            if first < 1:
                with eng.Fori(0, pairs) as r:
                    slot(r * 2 + 1, 1, True, True, True, r)
                    slot(r * 2 + 2, 0, True, True, True, r)
            for k in range(2 * pairs + 1, TILES + 1):
                slot(k, k & 1, True, k < TILES, k + 1 < TILES, (k - 1) // 2)

        chan_order = [("trx", 0, b) for b in range(2, 4)] + [("temp", -1, e) for e in range(4)] \
            + [("soma", 0, e) for e in range(4)] + [("trx", 1, b) for b in range(2)]
        tok_tail = [("n1", 0, 0)] + [("wg", 0, b) for b in range(4)] + [("tt", 0, b) for b in range(4)]
        tok_order = [("h", 1, 0)] + [item for b in range(4) for item in (("out", -1, b), ("y", 1, b))] + tok_tail
        tok_order_first = [("h", 1, 0)] + [("y", 1, b) for b in range(4)] + tok_tail
        tok_order_last = [("h", 1, 0)] + [("out", -1, b) for b in range(4)] + tok_tail
        read_by = {"h": h_ready, "temp": sg_ready, "n1": h1_ready, "soma": soma_ready, "trx": x1lo_ready,
                   "tt": tlo_ready, "out": out_copied, "y": y_ready, "wg": pre_ready}

        def tok_order_of(k):
            if isinstance(k, int) and k <= 0:
                return tok_order_first
            if isinstance(k, int) and k >= TILES - 1:
                return tok_order_last
            return tok_order

        def bank_of(order, banks, name, j):
            at = [n for n, (s, _, i) in enumerate(order) if (s, i) == (name, j)][0]
            return banks[at % len(banks)]

        def wait_bank(pe, order, banks, k, name, j):
            at = [n for n, (s, _, i) in enumerate(order) if (s, i) == (name, j)][0]
            while True:
                at -= len(banks)
                if at < 0:
                    at += len(order)
                    k = k - 1
                s, ahead, i = order[at]
                tile = k + ahead
                if isinstance(k, int):
                    if k < -1:
                        return
                    if not 0 <= tile < TILES:
                        continue
                pe.wait_ge(read_by[s], upto(names[s], tile, i))
                return

        block = ctx.enter_context(nc.Block())

        @block.sync
        def _(sp):
            def load_language(batch):
                one = sp.value_load(lang[0:1, bass.ds(batch, 1)], min_val=0, max_val=LANGS - 1)
                sp.dma_start(W1[:, :, :], w1[bass.ds(one, 1)].rearrange("a (n p) m -> p (a n) m", p=P)).then_inc(ld_lang, 16)
                sp.dma_start(W2[:, :], w2[bass.ds(one, 1)].rearrange("a p m -> p (a m)")).then_inc(ld_lang, 16)
                sp.dma_start(b1_col, b1[bass.ds(one, 1)].rearrange("a (p m) -> p (a m)", p=P)).then_inc(ld_lang, 16)
                for row, src in ((b2_row, b2), (gamma0_row, g0), (beta0_row, be0)):
                    sp.dma_start(row[:, :], src[bass.ds(one, 1)].to_broadcast([P, C])).then_inc(ld_lang, 16)

            def load_split(n, src, dst):
                sp.dma_start(dst, src.rearrange("(n p) m -> p n m", p=P)).then_inc(ld_split[n], 16)

            def load_x(tile):
                sp.dma_start(x_t[:, :, :], x[bass.ds(tile, 1)].rearrange("a (n p) c -> p (a n) c", p=P)).then_inc(ld_x, 16)

            def load_xT(tile):
                sp.dma_start(xT[:, :, :], xc[bass.ds(tile, 1)].rearrange("a (n p) t -> p (a n) t", p=P)).then_inc(ld_xT, 16)

            def first_loads():
                sp.dma_start(lang[:, :], ids).then_inc(ld_ids, 16)
                sp.dma_start(alpha[:, 0, :], taus).then_inc(ld_small, 16)
                sp.dma_start(blend_c, blend).then_inc(ld_small, 16)
                sp.dma_start(con, bits).then_inc(ld_small, 16)
                sp.dma_start(ident[:, :], eye).then_inc(ld_small, 16)
                sp.dma_start(col, cols).then_inc(ld_small, 16)
                sp.dma_start(bn2_row[:, :], bn2.to_broadcast([P, D])).then_inc(ld_small, 16)
                load_xT(0)
                sp.wait_ge(ld_ids, 16)
                load_language(0)
                load_x(0)
                load_split(0, wn1, stage[2])
                load_split(1, wsoma, stage[0])
                load_split(2, wg[0:C], stage[1])
                sp.dma_start(Wn2[:, :], wn2).then_inc(ld_rows, 16)
                for row, src in ((bg_row, bg), (gamma1_row, g1), (beta1_row, be1)):
                    sp.dma_start(row[:, :], src.to_broadcast([P, C])).then_inc(ld_rows, 16)

            def second_loads():
                sp.wait_ge(full["h"], 1)
                load_xT(1)
                sp.wait_ge(split_lo[1], 1)
                load_split(3, wg[C:2 * C], stage[0])
                sp.wait_ge(x1_ready, NB)
                load_x(1)
                sp.wait_ge(split_lo[2], 1)
                load_split(4, wtemp, stage[1])
                sp.dma_start(Wout[:, :, :], wout.rearrange("(n p) m -> p n m", p=P)).then_inc(ld_wout, 16)
                sp.dma_start(x1_dram[0], x1[0][:, :, :].rearrange("p b c -> p (b c)")).then_inc(x1_stored, 16)

            def slot(k, odd, has_prev, has_cur, has_next, r):
                if not has_prev:
                    second_loads()
                elif has_next:
                    if odd:
                        load_language(r + 1)
                    sp.wait_ge(U_ready, upto(PIECES, k - 1, 3 * PIECES // 4 - 1))
                    load_x(k + 1)
                    sp.wait_ge(U_ready, upto(PIECES, k - 1, PIECES - 1))
                    load_xT(k + 1)
                if has_prev:
                    if has_next:
                        sp.wait_ge(full["h"], upto(1, k + 1, 0))
                    else:
                        sp.wait_ge(U_ready, upto(PIECES, k - 1, PIECES - 1))
                    sp.dma_start(x1_back[:, :, :].rearrange("p b c -> p (b c)"), x1_dram[odd ^ 1]).then_inc(ld_back, 16)

                def store_result():
                    for b in range(NB):
                        sp.wait_ge(res_ready, upto(4, k - 1, b))
                        sp.dma_start(out_tiles[bass.ds(k - 1, 1), b * P:(b + 1) * P, :].rearrange("a p c -> p (a c)"),
                                     res[:, b, :]).then_inc(stored, 16)

                if not has_cur:
                    store_result()
                if has_cur:
                    for b in range(NB):
                        sp.wait_ge(g_ready, upto(4, k, b))
                        sp.dma_start(g_dram[b % 2].rearrange("s (i c) -> i s c", i=NI), g[:, b % 2, :]).then_inc(g_stored, 16)
                        if b == 1 and has_prev:
                            store_result()
                        sp.wait_ge(g_stored, 16 * upto(4, k, b))
                        for q in range(NQ):
                            sp.dma_start(grep[b % 2][q * L:(q + 1) * L, :, :].rearrange("p i c -> p (i c)"),
                                         g_dram[b % 2]).then_inc(grep_in[b % 2], 16)
                if has_next:
                    sp.wait_ge(x1_stored, 16 * upto(1, k, 0))
                    sp.dma_start(x1_dram[odd ^ 1], x1[odd ^ 1][:, :, :].rearrange("p b c -> p (b c)")).then_inc(x1_stored, 16)

            first_loads()
            run_slots(sp, slot, first=0)
            sp.wait_ge(stored, 16 * NB * TILES)
            sp.wait_ge(x1_stored, 16 * TILES)

        @block.gpsimd
        def _(pool):
            nc.gpsimd.memset(minus_half, -0.5).then_inc(half_ready, 1)
            pool.wait_ge(half_ready, 1)

            def slot(k, odd, has_prev, has_cur, has_next, r):
                if has_cur:
                    for n in range(NC):
                        if n == 0:
                            if has_prev:
                                pool.wait_ge(full["Uused"], upto(PIECES // 2, k - 1, PIECES // 2 - 1))
                            pool.wait_ge(x1lo_ready, upto(4, k, NB - 1))
                        if n == 0 and not has_prev:
                            pool.wait_ge(blend_spread, 1)
                        nc.gpsimd.tensor_tensor(ema[:, n, :], x1T[0][:, n, :].bitcast(F), x1T[1][:, n, :].bitcast(F),
                                                ALU.add).then_inc(whole_ready, 1)
                if has_next:
                    pool.wait_ge(ld_x, 16 * upto(1, k + 1, 0))
                    if odd:
                        pool.wait_ge(ld_lang, 96 * (r + 2))
                    for b in range(NB):
                        if has_prev:
                            pool.wait_ge(g_ready, upto(4, k - 1, b))
                            if b == 0:
                                pool.wait_ge(x1_stored, 16 * upto(1, k - 1, 0))
                        nc.gpsimd.tensor_tensor(x1[odd ^ 1][:, b, :], x_t[:, b, :], b2_row[:, :], ALU.add).then_inc(xb2_ready, 1)
                    for b in range(NB):
                        pool.wait_ge(xb2_ready, upto(4, k + 1, b))
                        nc.gpsimd.tensor_tensor(x_t[:, b, :], x_t[:, b, :], beta0_row[:, :], ALU.add).then_inc(xbeta_ready, 1)
                if has_prev:
                    pool.wait_ge(ld_back, 16 * upto(1, k - 1, 0))
                    if isinstance(k, int):
                        pool.wait_ge(ld_rows, 16 * 4)
                    for b in range(NB):
                        nc.gpsimd.tensor_tensor(x1_back[:, b, :], x1_back[:, b, :], beta1_row[:, :], ALU.add).then_inc(x1b_ready, 1)
                    pool.wait_ge(ln1_step, upto(13, k - 1, 8))
                    nc.gpsimd.tensor_tensor(rstd1, rstd1, minus_half, ALU.pow).then_inc(rstd1_ready, 1)
                if has_next:
                    pool.wait_ge(ln0_step, upto(13, k + 1, 8))
                    nc.gpsimd.tensor_tensor(rstd0, rstd0, minus_half, ALU.pow).then_inc(rstd0_ready, 1)
                    if not has_cur:
                        pool.wait_ge(split_hi, 2)
                        nc.gpsimd.tensor_tensor(Wsoma[1][:, :, :], stage[0], Wsoma[0][:, :, :].bitcast(F),
                                                ALU.subtract).then_inc(split_lo[1], 1)
                if has_prev:
                    for b in range(NB):
                        pool.wait_ge(scaled_ready, upto(4, k - 1, b))
                        pool.wait_ge(x1b_ready, upto(4, k - 1, b))
                        nc.gpsimd.tensor_tensor(res[:, b, :], res[:, b, :], x1_back[:, b, :], ALU.add).then_inc(res_ready, 1)

            run_slots(pool, slot)

        @block.scalar
        def _(act):
            def split(n, stage_n, dst):
                act.wait_ge(ld_split[n], 16)
                nc.scalar.activation(dst, stage[stage_n], ACT.Identity).then_inc(split_hi, 1)

            def slot(k, odd, has_prev, has_cur, has_next, r):
                def high(name, tile, b, ps, dst, ready):
                    act.wait_ge(full[name], upto(4, tile, b))
                    nc.scalar.activation(dst[0][:, :, b * P:(b + 1) * P],
                                         ps[:, :].rearrange("p (n t) -> p n t", n=NC),
                                         ACT.Identity).then_inc(ready, 1)

                def soma_gelu(e):
                    act.wait_ge(full["soma"], upto(4, k, e))
                    nc.scalar.activation(soma[:, e, :], bank_of(chan_order, chan, "soma", e)[:, :], ACT.Gelu,
                                         bias=col[:, 1 + e:2 + e]).then_inc(soma_ready, 1)

                def x1_high(tile, b):
                    high("trx", tile, b, bank_of(chan_order, chan, "trx", b), x1T, x1hi_ready)

                def trace_high(b):
                    high("tt", k, b, bank_of(tok_order, tokp, "tt", b), seq, thi_ready)

                if has_cur:
                    for b in range(2, NB):
                        x1_high(k, b)
                for e in range(NC):
                    if has_prev:
                        ps = bank_of(chan_order, chan, "temp", e)
                        act.wait_ge(full["temp"], upto(4, k - 1, e))
                        nc.scalar.activation(ps[:, :], ps[:, :], ACT.Sigmoid, bias=col[:, 5 + e:6 + e]).then_inc(gate_ready, 1)
                if has_next:
                    act.wait_ge(full["h"], upto(1, k + 1, 0))
                    nc.scalar.activation(hid[:, :], bank_of(tok_order_of(k), tokp, "h", 0)[:, :], ACT.Relu,
                                         bias=b1_col).then_inc(h_ready, 1)
                if has_cur:
                    for n in range(NC):
                        act.wait_ge(ema_ready, upto(4, k, n))
                        nc.scalar.activation(seq[0][:, n, :], ema[:, n, :], ACT.Identity).then_inc(emahi_ready, 1)
                if has_prev:
                    for b in range(NB):
                        act.wait_ge(full["out"], upto(4, k - 1, b))
                        nc.scalar.activation(res[:, b, :], bank_of(tok_order_of(k), tokp, "out", b)[:, :],
                                             ACT.Identity).then_inc(out_copied, 1)
                if has_cur:
                    if not has_prev:
                        split(3, 0, Wg[0][:, NC:2 * NC, :])
                    act.wait_ge(full["n1"], upto(1, k, 0))
                    nc.scalar.activation(hid[:, :], bank_of(tok_order_of(k), tokp, "n1", 0)[:, :], ACT.Gelu,
                                         bias=col[:, 0:1]).then_inc(h1_ready, 1)
                    if not has_prev:
                        act.wait_ge(split_lo[3], 1)
                    soma_gelu(0)
                    act.wait_ge(m_pre, upto(1, k, 0))
                    nc.scalar.activation(m_nat, m_nat, ACT.Sigmoid).then_inc(msig_ready, 1)

                if has_prev:
                    act.wait_ge(rstd1_ready, upto(1, k - 1, 0))
                    for b in range(NB):
                        act.wait_ge(ln1_step, upto(13, k - 1, 9 + b))
                        nc.scalar.activation(res[:, b, :], res[:, b, :], ACT.Identity, scale=rstd1[:, b:b + 1]).then_inc(scaled_ready, 1)

                def open_gate(b):
                    act.wait_ge(pre_ready, upto(4, k, b))
                    nc.scalar.activation(g[:, b % 2, :], g[:, b % 2, :], ACT.Sigmoid).then_inc(sig_ready, 1)

                def trace(b):
                    act.wait_ge(full["T"], upto(4, k, b))
                    nc.scalar.activation(T_sb[b % 2][:, :], Tp[b % 2][:, :], ACT.Identity).then_inc(T_ready, 1)

                if has_cur:
                    for b in range(3):
                        open_gate(b)
                        if b == 0 and not has_prev:
                            split(4, 1, Wtemp[0][:, :, :])
                    trace(0)
                    open_gate(3)
                    soma_gelu(1)
                    trace(1)
                    soma_gelu(2)
                    trace_high(0)
                    trace(2)
                    if not odd:
                        act.wait_ge(full["carry"], r + 2)
                        nc.scalar.activation(V[1][64:128, :], smp[64:128, :], ACT.Identity).then_inc(carry_ready, 1)
                    trace_high(1)
                    soma_gelu(3)
                    trace_high(2)
                    trace(3)
                if has_next:
                    if not has_cur:
                        split(0, 2, Wn1[0][:, :, :])
                        split(1, 0, Wsoma[0][:, :, :])
                        split(2, 1, Wg[0][:, 0:NC, :])
                    for b in range(2):
                        x1_high(k + 1, b)
                if has_cur:
                    trace_high(3)

            act.wait_ge(ld_small, 96)
            nc.scalar.activation(alpha[:, 0, :], alpha[:, 0, :], ACT.Exp).then_inc(setup_exp, 1)
            act.wait_ge(blend_ready, 1)
            nc.scalar.activation(blend_c, blend_c, ACT.Exp).then_inc(setup_exp, 1)
            act.wait_ge(blend_spread, 1)
            for hh in range(NH):
                nc.scalar.activation(w_qs[:, hh, :], Tp[hh][:, :], ACT.Identity)
            nc.scalar.activation(w_jd[:, :], smp[:, :], ACT.Identity).then_inc(setup_exp, 1)
            run_slots(act, slot)

        @block.vector
        def _(dve):
            steps = [0]

            def link(ins):
                steps[0] += 1
                ins.then_inc(setup_step, 1)
                dve.wait_ge(setup_step, steps[0])

            V_ = nc.vector

            def split(n, stage_n, dst):
                dve.wait_ge(split_hi, n + 1)
                V_.tensor_tensor(dst[1], stage[stage_n], dst[0].bitcast(F), ALU.subtract).then_inc(split_lo[n], 1)

            def small_tables():
                dve.wait_ge(ld_small, 96)
                link(V_.tensor_reduce(blend_s, blend_c, AX.X, ALU.max))
                V_.tensor_tensor(blend_c, blend_c, blend_s.unsqueeze(2).to_broadcast([P, NC, D]), ALU.subtract).then_inc(blend_ready, 1)
                dve.wait_ge(setup_exp, 1)
                link(V_.tensor_scalar(alpha[:, 0, :], alpha[:, 0, :], 1.0, None, ALU.add))
                link(V_.reciprocal(alpha[:, 0, :], alpha[:, 0, :]))
                V_.tensor_copy(alpha_ctx, alpha[:, 0, AL_CTX:AL_CTX + 1])
                dve.wait_ge(setup_exp, 2)
                link(V_.tensor_reduce(blend_s, blend_c, AX.X, ALU.add))
                link(V_.reciprocal(blend_s, blend_s))
                link(V_.tensor_tensor(blend_c, blend_c, blend_s.unsqueeze(2).to_broadcast([P, NC, D]), ALU.mult))
                for hh in range(NH):
                    for n in range(NC):
                        V_.tensor_copy(blend_x[:, hh, n, :].rearrange("p (q s) -> p q s", q=NQ),
                                       blend_c[:, n, hh * NQ:(hh + 1) * NQ].unsqueeze(2).to_broadcast([P, NQ, L]))
                for n in range(NC):
                    last = V_.tensor_copy(blend_x[:, 2, n, :].rearrange("p (j d) -> p j d", d=D),
                                          blend_c[:, n, :].unsqueeze(1).to_broadcast([P, SPANS, D]))
                last.then_inc(blend_ready, 1)

            def decay_tables():
                def bits_at(at, width):
                    return con[:, at:at + 5 * width].rearrange("p (n t) -> p n t", n=5)

                for n in range(1, LEVELS):
                    link(V_.tensor_tensor(alpha[:, n, :], alpha[:, n - 1, :], alpha[:, n - 1, :], ALU.mult))
                link(V_.tensor_scalar(alpha_1, alpha, 1.0, None, ALU.subtract))
                V_.tensor_tensor(factors[:, :, 0, :], bits_at(AT_TBITS, L),
                                 alpha_1[:, 0:5, AL_JD].unsqueeze(2).to_broadcast([P, 5, L]), ALU.mult)
                V_.tensor_tensor(factors[:, :, 1:3, :], bits_at(AT_DBITS, L).unsqueeze(2).to_broadcast([P, 5, NH, L]),
                                 alpha_1[:, 0:5, AL_Q:AL_Q + NH].unsqueeze(3).to_broadcast([P, 5, NH, L]), ALU.mult)
                V_.tensor_tensor(factors[:, :, 3, :], bits_at(AT_QBITS, 32),
                                 alpha_1[:, 5:10, AL_JD].unsqueeze(2).to_broadcast([P, 5, 32]), ALU.mult)
                link(V_.tensor_tensor(factors_s, alpha_1[:, 0:5, AL_ROW:AL_ROW + D],
                                      con[:, AT_RBITS:AT_RBITS + 5].unsqueeze(2).to_broadcast([P, 5, D]), ALU.mult))
                V_.tensor_tensor(factors_e, alpha_1[:, 5:10, AL_JD], con[:, AT_EBITS:AT_EBITS + 5], ALU.mult)
                link(V_.memset(Eend[:, :], 0.0))
                power, power_s, power_e = factors[:, 0, :, :], factors_s[:, 0, :], factors_e[:, 0:1]
                V_.tensor_scalar(power, power, 1.0, None, ALU.add)
                V_.tensor_scalar(power_e, power_e, 1.0, None, ALU.add)
                link(V_.tensor_scalar(power_s, power_s, 1.0, None, ALU.add))
                for n in range(1, 5):
                    V_.scalar_tensor_tensor(power, factors[:, n, :, :], 1.0, power, ALU.add, ALU.mult)
                    V_.scalar_tensor_tensor(power_e, factors_e[:, n:n + 1], 1.0, power_e, ALU.add, ALU.mult)
                    link(V_.scalar_tensor_tensor(power_s, factors_s[:, n, :], 1.0, power_s, ALU.add, ALU.mult))
                V_.tensor_tensor(Dpow[:, :, :], power[:, 1:3, :],
                                 con[:, AT_DMASK:AT_DMASK + L].unsqueeze(1).to_broadcast([P, NH, L]), ALU.mult)
                V_.tensor_scalar(Eend[:, L - D:L], con[:, AT_EMASK:AT_EMASK + D], power_e, None, ALU.mult)
                V_.tensor_tensor(Qpow, power[:, 3, :], con[:, AT_QMASK:AT_QMASK + 32], ALU.mult)
                link(V_.tensor_scalar(Tpow, power[:, 0, :], alpha[:, 0, AL_JD:AL_JD + 1], None, ALU.mult))
                V_.tensor_tensor(Epow[:, :, :].rearrange("p x (i t) -> p (x i) t", t=L), Qpow.unsqueeze(2).to_broadcast([P, 32, L]),
                                 Tpow.unsqueeze(1).to_broadcast([P, 32, L]), ALU.mult)
                V_.tensor_tensor(Rpow[:, :, :], power_s.unsqueeze(1).to_broadcast([P, NI, D]),
                                 con[:, AT_IMASK:AT_IMASK + NI].unsqueeze(2).to_broadcast([P, NI, D]),
                                 ALU.mult).then_inc(tables_ready, 1)
                dve.wait_ge(tables_ready, 1)

            def slot(k, odd, has_prev, has_cur, has_next, r):
                new = x1[odd ^ 1]

                def low(tile, b, ps, dst, hi_ready, ready):
                    dve.wait_ge(hi_ready, upto(4, tile, b))
                    at = slice(b * P, (b + 1) * P)
                    V_.tensor_tensor(dst[1][:, :, at], ps[:, :].rearrange("p (n t) -> p n t", n=NC),
                                     dst[0][:, :, at].bitcast(F), ALU.subtract).then_inc(ready, 1)

                def context(n):
                    if odd and n == 0:
                        dve.wait_ge(last_kept, upto(1, k - 1, 0))
                    dve.wait_ge(whole_ready, upto(4, k, n))
                    V_.tensor_tensor_scan(ema[:, n, :], alpha_ctx.to_broadcast([P, TOK]), ema[:, n, :],
                                          ema_last[:, n:n + 1] if odd else 0.0, ALU.mult, ALU.add).then_inc(ema_ready, 1)

                def x1_low(tile, b):
                    low(tile, b, bank_of(chan_order, chan, "trx", b), x1T, x1hi_ready, x1lo_ready)

                def trace_low(b):
                    low(k, b, bank_of(tok_order, tokp, "tt", b), seq, thi_ready, tlo_ready)

                if has_cur:
                    for b in range(2, NB):
                        x1_low(k, b)
                if has_cur and not has_prev:
                    split(0, 2, [w[:, :, :] for w in Wn1])
                    split(2, 1, [w[:, 0:NC, :] for w in Wg])
                for e in range(NC):
                    if has_prev:
                        dve.wait_ge(gate_ready, upto(4, k - 1, e))
                        V_.tensor_tensor(soma[:, e, :], bank_of(chan_order, chan, "temp", e)[:, :], soma[:, e, :],
                                         ALU.mult).then_inc(sg_ready, 1)
                    if has_cur and e:
                        context(e - 1)
                if has_cur:
                    context(NC - 1)
                    for n in range(NC):
                        dve.wait_ge(emahi_ready, upto(4, k, n))
                        V_.tensor_tensor(seq[1][:, n, :], ema[:, n, :], seq[0][:, n, :].bitcast(F), ALU.subtract).then_inc(emalo_ready, 1)
                    V_.tensor_copy(ema_last, ema[:, :, TOK - 1]).then_inc(last_kept, 1)

                def input_statistics(b):
                    dve.wait_ge(y_ready, upto(4, k + 1, b))
                    V_.bn_stats(stats0[:, b, :], new[:, b, :]).then_inc(ln0_step, 1)

                for b in range(NB):
                    if has_prev:
                        dve.wait_ge(out_copied, upto(4, k - 1, b))
                        V_.bn_stats(stats1[:, b, :], res[:, b, :]).then_inc(ln1_step, 1)
                    if has_next:
                        dve.wait_ge(full["y"], upto(4, k + 1, b))
                        dve.wait_ge(xb2_ready, upto(4, k + 1, b))
                        V_.tensor_tensor(new[:, b, :], bank_of(tok_order_of(k), tokp, "y", b)[:, :], new[:, b, :],
                                         ALU.add).then_inc(y_ready, 1)
                        if b:
                            if b == NB - 1 and has_prev:
                                dve.wait_ge(ln1_step, upto(13, k - 1, NB - 1))
                            input_statistics(b - 1)
                if has_next:
                    input_statistics(NB - 1)
                if has_cur and not has_prev:
                    split(3, 0, [w[:, NC:2 * NC, :] for w in Wg])
                if has_prev:
                    for b in range(NB):
                        if isinstance(k, int):
                            dve.wait_ge(ln1_step, upto(13, k - 1, b))
                        V_.bn_aggr(mv1[:, b, :], stats1[:, b, :]).then_inc(ln1_step, 1)
                    dve.wait_ge(ln1_step, upto(13, k - 1, 7))
                    V_.tensor_scalar(rstd1, mv1[:, :, 1], EPS, None, ALU.add).then_inc(ln1_step, 1)
                    for b in range(NB):
                        if b == NB - 1 and has_next:
                            dve.wait_ge(ln0_step, upto(13, k + 1, NB - 1))
                        V_.scalar_tensor_tensor(res[:, b, :], res[:, b, :], mv1[:, b, 0:1], gamma1_row[:, :],
                                                ALU.subtract, ALU.mult).then_inc(ln1_step, 1)
                if has_next:
                    for b in range(NB):
                        if isinstance(k, int):
                            dve.wait_ge(ln0_step, upto(13, k + 1, b))
                        V_.bn_aggr(mv0[:, b, :], stats0[:, b, :]).then_inc(ln0_step, 1)
                    dve.wait_ge(ln0_step, upto(13, k + 1, 7))
                    V_.tensor_scalar(rstd0, mv0[:, :, 1], EPS, None, ALU.add).then_inc(ln0_step, 1)
                if has_cur:
                    dve.wait_ge(full["m"], upto(1, k, 0))
                    V_.tensor_tensor(m_nat, smp[:, 0:NB * D].rearrange("p (b d) -> p b d", b=NB),
                                     bn2_row[:, :].unsqueeze(1).to_broadcast([P, NB, D]), ALU.add).then_inc(m_pre, 1)
                if has_next:
                    for b in range(NB):
                        V_.scalar_tensor_tensor(new[:, b, :], new[:, b, :], mv0[:, b, 0:1], gamma0_row[:, :],
                                                ALU.subtract, ALU.mult).then_inc(ln0_step, 1)

                def input_normed():
                    dve.wait_ge(rstd0_ready, upto(1, k + 1, 0))
                    for b in range(NB):
                        dve.wait_ge(ln0_step, upto(13, k + 1, 9 + b))
                        dve.wait_ge(xbeta_ready, upto(4, k + 1, b))
                        V_.scalar_tensor_tensor(new[:, b, :], new[:, b, :], rstd0[:, b:b + 1], x_t[:, b, :],
                                                ALU.mult, ALU.add).then_inc(x1_ready, 1)

                if has_cur:
                    dve.wait_ge(msig_ready, upto(1, k, 0))
                    V_.tensor_scalar(m_nat, m_nat, 0.5, None, ALU.add).then_inc(m_ready, 1)
                if has_next:
                    input_normed()
                if has_cur:
                    dve.wait_ge(m_ready, upto(1, k, 0))
                    V_.tensor_tensor(Bm[:, :, :, :], m_nat.unsqueeze(2).to_broadcast([P, NB, NI, D]),
                                     Rpow[:, :, :].unsqueeze(1).to_broadcast([P, NB, NI, D]), ALU.mult).then_inc(Bm_ready, 1)

                    def products(b, hh):
                        for c in range(2):
                            n = 4 * b + 2 * hh + c
                            if b == 0 and hh == 0 and c == 0:
                                dve.wait_ge(A_ready, upto(1, k, 0))
                            if hh == 0 and c == 0:
                                dve.wait_ge(grep_in[b % 2], 64 * upto(2, k, b // 2))
                            if c == 0 and b == 0:
                                if has_prev and hh == 1:
                                    dve.wait_ge(stored, 16 * upto(4, k - 1, NB - 1))
                            elif c == 0:
                                dve.wait_ge(full["Uused"], upto(PIECES // 2, k, n // 2 - 2))
                            at = slice(c * HC, (c + 1) * HC)
                            V_.tensor_tensor(U[:, (n + 2) % 4, :, :], grep[b % 2][:, :, at],
                                             w_qs[:, hh, at].unsqueeze(1).to_broadcast([P, NI, HC]), ALU.mult).then_inc(U_ready, 1)

                    def gate_logits(b):
                        dve.wait_ge(full["wg"], upto(4, k, b))
                        if b == 2:
                            dve.wait_ge(full["S"], upto(2, k, 0))
                        V_.tensor_tensor(g[:, b % 2, :], bank_of(tok_order_of(k), tokp, "wg", b)[:, :], bg_row[:, :],
                                         ALU.add).then_inc(pre_ready, 1)

                    def gated(b):
                        dve.wait_ge(sig_ready, upto(4, k, b))
                        V_.tensor_tensor(g[:, b % 2, :], g[:, b % 2, :], x1[odd][:, b, :], ALU.mult).then_inc(g_ready, 1)

                    def span_states(half):
                        rows = slice(half * 64, half * 64 + (64 - D if odd and half else 64))
                        dve.wait_ge(full["S"], upto(2, k, half))
                        V_.tensor_tensor(V[odd][rows, :], smp[rows, :], w_jd[rows, :], ALU.mult).then_inc(V_ready, 1)

                    if not has_prev:
                        dve.wait_ge(ld_rows, 16 * 4)
                    gate_logits(0)
                    dve.wait_ge(full["mrep"], upto(1, k, 0))
                    V_.tensor_copy(m_rep.rearrange("p (b i) h -> p b i h", b=NB),
                                   smp[:, 32:32 + NI * NB * NH].rearrange("p (i b h) -> p b i h", i=NI, b=NB)).then_inc(mrep_ready, 1)
                    gated(0)
                    if not has_prev:
                        split(4, 1, [w[:, :, :] for w in Wtemp])
                        dve.wait_ge(setup_exp, 3)
                    dve.wait_ge(mrep_ready, upto(1, k, 0))
                    V_.tensor_tensor(Arep[:, :, :, :],
                                     m_rep.unsqueeze(3).to_broadcast([P, NB * NI, NH, L]),
                                     Dpow[:, :, :].unsqueeze(1).to_broadcast([P, NB * NI, NH, L]),
                                     ALU.mult).then_inc(A_ready, 1)
                    gate_logits(1)
                    gated(1)
                    products(0, 0)
                    span_states(0)
                    gate_logits(2)
                    products(0, 1)
                    gated(2)
                    products(1, 0)
                    products(1, 1)
                    gate_logits(3)
                    gated(3)
                    products(2, 0)
                    span_states(1)
                    products(2, 1)
                    trace_low(0)
                    products(3, 0)
                    products(3, 1)
                    trace_low(1)
                    trace_low(2)
                if has_next:
                    for b in range(2):
                        x1_low(k + 1, b)
                if has_cur:
                    trace_low(3)

            small_tables()
            decay_tables()
            run_slots(dve, slot)

        @block.tensor
        def _(pe):
            def product(dst, lhsT, rhs, steps, signal):
                for n in range(steps):
                    last = nc.tensor.matmul(dst, lhsT(n), rhs(n), start=(n == 0), stop=(n == steps - 1))
                last.then_inc(full[signal], 1)

            def split_product(dst, lhsT, rhs, steps, first=True, final=True):
                for n in range(steps):
                    for m, (a, b) in enumerate(((0, 0), (0, 1), (1, 0))):
                        last = nc.tensor.matmul(dst, lhsT(a, n), rhs(b, n), start=(first and n == 0 and m == 0),
                                                stop=(final and n == steps - 1 and m == 2))
                return last

            def slot(k, odd, has_prev, has_cur, has_next, r):
                def chan_bank(name, j):
                    wait_bank(pe, chan_order, chan, k, name, j)
                    return bank_of(chan_order, chan, name, j)

                def tok_bank(name, j):
                    wait_bank(pe, tok_order_of(k), tokp, k, name, j)
                    return bank_of(tok_order_of(k), tokp, name, j)

                def x1_by_channels(tile, new, b):
                    ps = chan_bank("trx", b)
                    pe.wait_ge(x1_ready, upto(4, tile, b))
                    for n in range(NC):
                        last = nc.tensor.transpose(ps[:, n * P:(n + 1) * P], new[:, b, n * P:(n + 1) * P], ident[:, :])
                    last.then_inc(full["trx"], 1)

                def temporal_gate(e):
                    ps = chan_bank("temp", e)
                    if e == 0:
                        pe.wait_ge(tlo_ready, upto(4, k - 1, NB - 1))
                        if isinstance(k, int):
                            pe.wait_ge(split_lo[4], 1)
                    at = slice(e * P, (e + 1) * P)
                    split_product(ps[:, :], lambda a, n: Wtemp[a][:, n, at], lambda a, n: seq[a][:, n, :],
                                  NC).then_inc(full["temp"], 1)

                def soma_of(e):
                    ps = chan_bank("soma", e)
                    at = slice(e * P, (e + 1) * P)
                    split_product(ps[:, :], lambda a, n: Wsoma[a][:, n, at], lambda a, n: x1T[a][:, n, :],
                                  NC).then_inc(full["soma"], 1)

                if has_cur:
                    for b in range(2, NB):
                        x1_by_channels(k, x1[odd], b)
                for e in range(NC):
                    if has_prev:
                        temporal_gate(e)
                if has_next:
                    pe.wait_ge(ld_xT, 16 * upto(1, k + 1, 0))
                    if odd:
                        pe.wait_ge(ld_lang, 96 * (r + 2))
                    ps = tok_bank("h", 0)
                    product(ps[:, :], lambda n: W1[:, n, :], lambda n: xT[:, n, :], NC, "h")
                for b in range(NB):
                    if has_prev:
                        if b == 0:
                            pe.wait_ge(sg_ready, upto(4, k - 1, NC - 1))
                            if isinstance(k, int):
                                pe.wait_ge(ld_wout, 16)
                        ps = tok_bank("out", b)
                        product(ps[:, :], lambda n: soma[:, n, b * P:(b + 1) * P], lambda n: Wout[:, n, :], NC, "out")
                    if has_next:
                        if b == 0:
                            pe.wait_ge(h_ready, upto(1, k + 1, 0))
                        ps = tok_bank("y", b)
                        product(ps[:, :], lambda n: hid[:, b * P:(b + 1) * P], lambda n: W2[:, :], 1, "y")
                if has_cur:
                    ps = tok_bank("n1", 0)
                    pe.wait_ge(x1lo_ready, upto(4, k, NB - 1))
                    if not has_prev:
                        pe.wait_ge(split_lo[0], 1)
                    split_product(ps[:, :], lambda a, n: Wn1[a][:, n, :], lambda a, n: x1T[a][:, n, :], NC).then_inc(full["n1"], 1)
                    if not has_prev:
                        pe.wait_ge(split_lo[1], 1)
                    soma_of(0)
                    pe.wait_ge(h1_ready, upto(1, k, 0))
                    if has_prev:
                        pe.wait_ge(V_ready, upto(2, k - 1, 1))
                        if odd:
                            pe.wait_ge(carry_ready, r + 1)
                    else:
                        pe.wait_ge(setup_exp, 3)
                        pe.wait_ge(ld_rows, 16 * 4)
                    for b in range(NB):
                        last = nc.tensor.matmul(smp[:, b * D:(b + 1) * D], hid[:, b * P:(b + 1) * P], Wn2[:, :],
                                                start=True, stop=True)
                    last.then_inc(full["m"], 1)
                    if not has_prev:
                        pe.wait_ge(split_lo[2], 1)
                        pe.wait_ge(split_lo[3], 1)
                    pe.wait_ge(emalo_ready, upto(4, k, NC - 1))

                def value_gate(b, part):
                    ps = tok_bank("wg", b) if part == 0 else bank_of(tok_order_of(k), tokp, "wg", b)
                    src, at = (x1T, seq)[part], slice(b * P, (b + 1) * P)
                    last = split_product(ps[:, :], lambda a, n: src[a][:, n, at], lambda a, n: Wg[a][:, part * NC + n, :],
                                         NC, first=part == 0, final=part == 1)
                    if part:
                        last.then_inc(full["wg"], 1)

                def spread_modulation():
                    pe.wait_ge(m_ready, upto(1, k, 0))
                    for i in range(NI):
                        for q in range(NQ):
                            last = nc.tensor.matmul(smp[q * L:(q + 1) * L, 32 + 8 * i:40 + 8 * i], ident[:, i * L:(i + 1) * L],
                                                    U[:, 3, NI - 1, q:NB * D:NQ], start=True, stop=True)
                    last.then_inc(full["mrep"], 1)

                def span_states(half):
                    pe.wait_ge(g_ready, upto(4, k, 2 * half + 1))
                    if half == 0:
                        pe.wait_ge(Bm_ready, upto(1, k, 0))
                        pe.wait_ge(mrep_ready, upto(1, k, 0))
                    for b in (2 * half, 2 * half + 1):
                        last = nc.tensor.matmul(smp[b * 32:(b + 1) * 32, :], Bm[:, b, :, :].rearrange("p i d -> p (i d)"),
                                                g[:, b % 2, :], start=True, stop=True)
                    last.then_inc(full["S"], 1)

                def within_spans(b, hh):
                    if b == 0 and hh == 0:
                        pe.wait_ge(A_ready, upto(1, k, 0))
                    if hh == 0:
                        if b >= 2 or has_prev:
                            pe.wait_ge(T_ready, upto(4, k, b - 2))
                        elif b == 0:
                            pe.wait_ge(setup_exp, 3)
                    for c in range(2):
                        n = 4 * b + 2 * hh + c
                        pe.wait_ge(U_ready, upto(PIECES, k, n))
                        at = slice(c * HC, (c + 1) * HC)
                        for i in range(NI):
                            last = nc.tensor.matmul(Tp[b % 2][i * L:(i + 1) * L, at], Arep[:, b * NI + i, hh, :],
                                                    U[:, (n + 2) % 4, i, :], start=(hh == 0 and c == 0), stop=False)
                    last.then_inc(full["Uused"], 1)

                def from_before(b):
                    if b == 0 and not has_prev:
                        pe.wait_ge(tables_ready, 1)
                    pe.wait_ge(V_ready, upto(2, k, b // 2))
                    rows = slice(0, 128 if b >= 2 else 96 if odd else 64)
                    nc.tensor.matmul(Tp[b % 2][:, :], Epow[rows, odd * NB + b, :], V[odd][rows, :],
                                     start=False, stop=True).then_inc(full["T"], 1)

                def tile_state():
                    nc.tensor.matmul(smp[64:96, :], Eend[:, L - D:2 * L - D], V[0][:, :], start=True, stop=True)
                    nc.tensor.matmul(smp[96:128, :], Eend[:, 0:L], V[0][:, :], start=True, stop=True).then_inc(full["carry"], 1)

                def trace_by_channels(b):
                    ps = tok_bank("tt", b)
                    pe.wait_ge(T_ready, upto(4, k, b))
                    for n in range(NC):
                        last = nc.tensor.transpose(ps[:, n * P:(n + 1) * P], T_sb[b % 2][:, n * P:(n + 1) * P], ident[:, :])
                    last.then_inc(full["tt"], 1)

                if has_cur:
                    value_gate(0, 0)
                    value_gate(0, 1)
                    spread_modulation()
                    value_gate(1, 0)
                    value_gate(1, 1)
                    value_gate(2, 0)
                    span_states(0)
                    value_gate(2, 1)
                    within_spans(0, 0)
                    value_gate(3, 0)
                    within_spans(0, 1)
                    from_before(0)
                    value_gate(3, 1)
                    within_spans(1, 0)
                    soma_of(1)
                    within_spans(1, 1)
                    from_before(1)
                    span_states(1)
                    soma_of(2)
                    within_spans(2, 0)
                    trace_by_channels(0)
                    within_spans(2, 1)
                    from_before(2)
                    if not odd:
                        tile_state()
                    trace_by_channels(1)
                    soma_of(3)
                    within_spans(3, 0)
                    trace_by_channels(2)
                    within_spans(3, 1)
                    from_before(3)
                if has_next:
                    for b in range(2):
                        x1_by_channels(k + 1, x1[odd ^ 1], b)
                if has_cur:
                    trace_by_channels(3)

            pe.wait_ge(ld_small, 96)
            pe.wait_ge(blend_ready, 2)
            for n in range(NC):
                at = slice(n * P, (n + 1) * P)
                for hh in range(NH):
                    nc.tensor.transpose(Tp[hh][:, at], blend_x[:, hh, n, :], ident[:, :])
                last = nc.tensor.transpose(smp[:, at], blend_x[:, 2, n, :], ident[:, :])
            last.then_inc(blend_spread, 1)
            run_slots(pe, slot)


def shape_constants():
    import numpy as np

    r = np.arange(P)
    con = np.zeros((P, BITS), np.float32)
    t = np.arange(32)

    def bits(at, n):
        n = np.clip(n, 0, 31)
        for k in range(5):
            con[:, at + 32 * k:at + 32 * (k + 1)] = (n >> k) & 1

    d = t[None, :] - (r % L)[:, None]
    bits(AT_DBITS, d)
    con[:, AT_DMASK:AT_DMASK + L] = d >= 0
    x, j = (t % SPANS)[None, :], (r // D)[:, None]
    n = np.where((t[None, :] >= SPANS) & (j == np.where(x < SPANS // 2, SPANS // 2, SPANS - 1)), x, x - j - 1)
    bits(AT_QBITS, n)
    con[:, AT_QMASK:AT_QMASK + 32] = n >= 0
    bits(AT_TBITS, np.broadcast_to(t[None, :], (P, 32)))
    for k in range(5):
        con[:, AT_RBITS + k] = ((L - 1 - r % L) >> k) & 1
    con[:, AT_IMASK:AT_IMASK + NI] = (r // L)[:, None] == np.arange(NI)[None, :]
    for k in range(5):
        con[:, AT_EBITS + k] = ((SPANS - 1 - r // D) >> k) & 1
    con[:, AT_EMASK:AT_EMASK + D] = (r % D)[:, None] == np.arange(D)[None, :]
    return con


def kernel(x, itok_B_0_8, condB_tauraws, cond_256, condB_bn2, cond_1024, L0_cond_W1, L0_cond_b1, L0_cond_W2,
           L0_cond_b2, L0_cond_gamma, L0_cond_beta, L1_cond_tau_ctx, L1_cond_Wg, L1_cond_bg, L1_cond_Wn1,
           L1_cond_bn1, L1_cond_Wsoma, L1_cond_bsoma, L1_cond_Wtemp, L1_cond_btemp, L1_cond_Wout,
           L1_cond_gamma, L1_cond_beta):
    import numpy as np
    import concourse.bacc as bacc
    from concourse.bass_utils import run_bass_kernel_spmd

    c = np.ascontiguousarray
    x = np.asarray(x)
    xs = x.reshape(TILES, TOK, C)
    taus = np.asarray(condB_tauraws)
    rows = np.arange(P)
    tau_table = np.concatenate([taus[rows % D][:, None], taus[rows // L][:, None], taus[NQ + rows // L][:, None],
                                np.broadcast_to(taus[None, :], (P, D)),
                                np.broadcast_to(np.asarray(L1_cond_tau_ctx).reshape(1, 1), (P, 1))], axis=1)
    by_chunk = lambda v: np.asarray(v).reshape(NC, P).T
    cols = np.concatenate([np.asarray(L1_cond_bn1)[:, None], by_chunk(L1_cond_bsoma), by_chunk(L1_cond_btemp)], axis=1)
    arrays = {
        "x": c(xs), "xc": c(xs.transpose(0, 2, 1)), "ids": np.asarray(itok_B_0_8).reshape(1, BATCHES),
        "w1": c(L0_cond_W1), "w2": c(L0_cond_W2), "b1": c(L0_cond_b1), "b2": c(L0_cond_b2),
        "g0": c(L0_cond_gamma), "be0": c(L0_cond_beta),
        "wg": c(np.asarray(L1_cond_Wg).T), "wn1": c(np.asarray(L1_cond_Wn1).T), "wsoma": c(np.asarray(L1_cond_Wsoma).T),
        "wtemp": c(np.asarray(L1_cond_Wtemp).T), "wout": c(np.asarray(L1_cond_Wout).T), "wn2": c(np.asarray(cond_256).T),
        "bg": np.asarray(L1_cond_bg).reshape(1, C), "g1": np.asarray(L1_cond_gamma).reshape(1, C),
        "be1": np.asarray(L1_cond_beta).reshape(1, C), "cols": c(cols), "taus": c(tau_table),
        "bn2": np.asarray(condB_bn2).reshape(1, D),
        "blend": c(np.asarray(cond_1024).reshape(D, NC, P).transpose(2, 1, 0)),
        "eye": np.eye(P, dtype=np.float32), "bits": shape_constants(),
    }
    nc = bacc.Bacc("TRN2", target_bir_lowering=False, num_devices=1)
    args = {n: nc.dram_tensor(f"in_{n}", a.shape, mybir.dt.from_np(a.dtype), kind="ExternalInput").ap()
            for n, a in arrays.items()}
    out = nc.dram_tensor("out", (BATCHES, SEQ, C), mybir.dt.float32, kind="ExternalOutput").ap()
    cond_resid_kernel(nc, out=out, **args)
    r = run_bass_kernel_spmd(nc, [{f"in_{n}": a for n, a in arrays.items()}], core_ids=[0])
    return r.results[0]["out"]
```
